# Optimizing a Trainium2 kernel written in Bass

```python
import numpy as np
import jax
import jax.numpy as jnp

def _softmax(x, axis=-1):
    return jax.nn.softmax(x, axis=axis)

def _gelu(x):
    return jax.nn.gelu(x, approximate=True)

def _silu(x):
    return jax.nn.silu(x)

def _sigmoid(x):
    return jax.nn.sigmoid(x)

def _layernorm(x, axis=-1, eps=1e-05):
    m = jnp.mean(x, axis=axis, keepdims=True)
    v = jnp.var(x, axis=axis, keepdims=True)
    return (x - m) / jnp.sqrt(v + eps)

def _scatter_add(tgt, idx, src, axis=0):
    return tgt.at[idx].add(src)

def _segment_sum(src, seg, n):
    return jax.ops.segment_sum(src, seg, n)
kernel_name = 'mk_sandwich_d2_jaxref_r8_45d5af'

def setup_inputs(seed: int=0):
    np.random.seed(seed)
    _w = jnp.asarray

    def _L0_attn_setup():
        import jax, jax.numpy as jnp
        import numpy as np
        D_MODEL = 256
        N_HEADS = 16
        D_HEAD = D_MODEL // N_HEADS
        D_Q = D_MODEL // 3
        D_KV = D_MODEL // 2
        D_QK_N = D_HEAD // 2
        D_QK_R = D_HEAD // 2
        EPS = 1e-05

        def _layernorm(x, g, b):
            mu = jnp.mean(x, axis=-1, keepdims=True)
            var = jnp.var(x, axis=-1, keepdims=True)
            return (x - mu) * jax.lax.rsqrt(var + EPS) * g + b

        def _rotary(x):
            d = x.shape[-1]
            inv_freq = (1.0 / 10000.0) ** (jnp.arange(0, d, 2, dtype=jnp.float32) / d)
            t = jnp.arange(x.shape[1], dtype=jnp.float32)
            freqs = t[:, None] * inv_freq[None, :]
            cos = jnp.cos(freqs)[None, :, None, :]
            sin = jnp.sin(freqs)[None, :, None, :]
            x1, x2 = jnp.split(x, 2, axis=3)
            return jnp.concatenate([x1 * cos + x2 * sin, -x1 * sin + x2 * cos], axis=3)
        key = jax.random.key(seed)
        ks = jax.random.split(key, 16)
        s = 0.02
        inp = {'x': jax.random.normal(ks[0], (2, 256, D_MODEL), dtype=jnp.float32), 'W_d_q': jax.random.normal(ks[1], (D_Q, D_MODEL), dtype=jnp.float32) * s, 'b_d_q': jnp.zeros((D_Q,), jnp.float32), 'q_norm_g': jnp.ones((D_Q,), jnp.float32), 'q_norm_b': jnp.zeros((D_Q,), jnp.float32), 'W_u_q': jax.random.normal(ks[2], (D_MODEL, D_Q), dtype=jnp.float32) * s, 'b_u_q': jnp.zeros((D_MODEL,), jnp.float32), 'W_d_kv': jax.random.normal(ks[3], (D_KV + D_QK_R, D_MODEL), dtype=jnp.float32) * s, 'b_d_kv': jnp.zeros((D_KV + D_QK_R,), jnp.float32), 'kv_norm_g': jnp.ones((D_KV,), jnp.float32), 'kv_norm_b': jnp.zeros((D_KV,), jnp.float32), 'W_u_kv': jax.random.normal(ks[4], (D_MODEL + N_HEADS * D_QK_N, D_KV), dtype=jnp.float32) * s, 'b_u_kv': jnp.zeros((D_MODEL + N_HEADS * D_QK_N,), jnp.float32), 'W_o': jax.random.normal(ks[5], (D_MODEL, D_MODEL), dtype=jnp.float32) * s, 'b_o': jnp.zeros((D_MODEL,), jnp.float32)}
        return inp
    _L0_attn_in = _L0_attn_setup()

    def _L0_ffn_setup():
        import jax, jax.numpy as jnp
        import numpy as np
        HIDDEN = 256
        INTER = 1024
        B, S = (4, 128)

        def _qmatmul(x, w_int8, scale):
            y = jnp.einsum('bsh,ho->bso', x, w_int8.astype(x.dtype))
            return y * scale
        key = jax.random.key(seed)
        ks = jax.random.split(key, 7)
        x = jax.random.normal(ks[0], (B, S, HIDDEN), dtype=jnp.float32)
        w_gate = jax.random.randint(ks[1], (HIDDEN, INTER), -128, 128, dtype=jnp.int32).astype(jnp.int8)
        w_up = jax.random.randint(ks[2], (HIDDEN, INTER), -128, 128, dtype=jnp.int32).astype(jnp.int8)
        w_down = jax.random.randint(ks[3], (INTER, HIDDEN), -128, 128, dtype=jnp.int32).astype(jnp.int8)
        s_gate = jax.random.uniform(ks[4], (INTER,), dtype=jnp.float32) * 0.02 + 0.001
        s_up = jax.random.uniform(ks[5], (INTER,), dtype=jnp.float32) * 0.02 + 0.001
        s_down = jax.random.uniform(ks[6], (HIDDEN,), dtype=jnp.float32) * 0.02 + 0.001
        return {'x': x, 'w_gate': w_gate, 'w_up': w_up, 'w_down': w_down, 's_gate': s_gate, 's_up': s_up, 's_down': s_down}
    _L0_ffn_in = _L0_ffn_setup()

    def _L1_attn_setup():
        import jax, jax.numpy as jnp
        import numpy as np
        import math
        D_MODEL = 256
        NUM_HEADS = 16
        HEAD_DIM = D_MODEL // NUM_HEADS
        key = jax.random.key(seed)
        k_x, k_wqkv, k_bqkv, k_wo, k_bo = jax.random.split(key, 5)
        B, S = (2, 256)
        scale = 1.0 / math.sqrt(D_MODEL)
        return {'x': jax.random.normal(k_x, (B, S, D_MODEL), dtype=jnp.float32), 'w_qkv': jax.random.normal(k_wqkv, (3 * D_MODEL, D_MODEL), dtype=jnp.float32) * scale, 'b_qkv': jax.random.normal(k_bqkv, (3 * D_MODEL,), dtype=jnp.float32) * 0.01, 'w_out': jax.random.normal(k_wo, (D_MODEL, D_MODEL), dtype=jnp.float32) * scale, 'b_out': jax.random.normal(k_bo, (D_MODEL,), dtype=jnp.float32) * 0.01}
    _L1_attn_in = _L1_attn_setup()

    def _L1_ffn_setup():
        import jax, jax.numpy as jnp
        import numpy as np
        HIDDEN = 256
        INTER = 1024
        B, S = (4, 128)

        def _qmatmul(x, w_int8, scale):
            y = jnp.einsum('bsh,ho->bso', x, w_int8.astype(x.dtype))
            return y * scale
        key = jax.random.key(seed)
        ks = jax.random.split(key, 7)
        x = jax.random.normal(ks[0], (B, S, HIDDEN), dtype=jnp.float32)
        w_gate = jax.random.randint(ks[1], (HIDDEN, INTER), -128, 128, dtype=jnp.int32).astype(jnp.int8)
        w_up = jax.random.randint(ks[2], (HIDDEN, INTER), -128, 128, dtype=jnp.int32).astype(jnp.int8)
        w_down = jax.random.randint(ks[3], (INTER, HIDDEN), -128, 128, dtype=jnp.int32).astype(jnp.int8)
        s_gate = jax.random.uniform(ks[4], (INTER,), dtype=jnp.float32) * 0.02 + 0.001
        s_up = jax.random.uniform(ks[5], (INTER,), dtype=jnp.float32) * 0.02 + 0.001
        s_down = jax.random.uniform(ks[6], (HIDDEN,), dtype=jnp.float32) * 0.02 + 0.001
        return {'x': x, 'w_gate': w_gate, 'w_up': w_up, 'w_down': w_down, 's_gate': s_gate, 's_up': s_up, 's_down': s_down}
    _L1_ffn_in = _L1_ffn_setup()
    _d = {'L0_attn_x': _L0_attn_in['x'], 'L0_attn_W_d_q': _L0_attn_in['W_d_q'], 'L0_attn_b_d_q': _L0_attn_in['b_d_q'], 'L0_attn_q_norm_g': _L0_attn_in['q_norm_g'], 'L0_attn_q_norm_b': _L0_attn_in['q_norm_b'], 'L0_attn_W_u_q': _L0_attn_in['W_u_q'], 'L0_attn_b_u_q': _L0_attn_in['b_u_q'], 'L0_attn_W_d_kv': _L0_attn_in['W_d_kv'], 'L0_attn_b_d_kv': _L0_attn_in['b_d_kv'], 'L0_attn_kv_norm_g': _L0_attn_in['kv_norm_g'], 'L0_attn_kv_norm_b': _L0_attn_in['kv_norm_b'], 'L0_attn_W_u_kv': _L0_attn_in['W_u_kv'], 'L0_attn_b_u_kv': _L0_attn_in['b_u_kv'], 'L0_attn_W_o': _L0_attn_in['W_o'], 'L0_attn_b_o': _L0_attn_in['b_o'], 'L0_ffn_w_gate': _L0_ffn_in['w_gate'], 'L0_ffn_w_up': _L0_ffn_in['w_up'], 'L0_ffn_w_down': _L0_ffn_in['w_down'], 'L0_ffn_s_gate': _L0_ffn_in['s_gate'], 'L0_ffn_s_up': _L0_ffn_in['s_up'], 'L0_ffn_s_down': _L0_ffn_in['s_down'], 'L1_attn_w_qkv': _L1_attn_in['w_qkv'], 'L1_attn_b_qkv': _L1_attn_in['b_qkv'], 'L1_attn_w_out': _L1_attn_in['w_out'], 'L1_attn_b_out': _L1_attn_in['b_out'], 'L1_ffn_w_gate': _L1_ffn_in['w_gate'], 'L1_ffn_w_up': _L1_ffn_in['w_up'], 'L1_ffn_w_down': _L1_ffn_in['w_down'], 'L1_ffn_s_gate': _L1_ffn_in['s_gate'], 'L1_ffn_s_up': _L1_ffn_in['s_up'], 'L1_ffn_s_down': _L1_ffn_in['s_down']}
    _x0 = _d['L0_attn_x']
    _d['L0_attn_x'] = jax.random.normal(jax.random.fold_in(jax.random.key(seed), 1), (1, 2048, 256), dtype=_x0.dtype)
    del _x0
    return _d

def reference(L0_attn_x, L0_attn_W_d_q, L0_attn_b_d_q, L0_attn_q_norm_g, L0_attn_q_norm_b, L0_attn_W_u_q, L0_attn_b_u_q, L0_attn_W_d_kv, L0_attn_b_d_kv, L0_attn_kv_norm_g, L0_attn_kv_norm_b, L0_attn_W_u_kv, L0_attn_b_u_kv, L0_attn_W_o, L0_attn_b_o, L0_ffn_w_gate, L0_ffn_w_up, L0_ffn_w_down, L0_ffn_s_gate, L0_ffn_s_up, L0_ffn_s_down, L1_attn_w_qkv, L1_attn_b_qkv, L1_attn_w_out, L1_attn_b_out, L1_ffn_w_gate, L1_ffn_w_up, L1_ffn_w_down, L1_ffn_s_gate, L1_ffn_s_up, L1_ffn_s_down):

    def _L0_attn_ref(x, W_d_q, b_d_q, q_norm_g, q_norm_b, W_u_q, b_u_q, W_d_kv, b_d_kv, kv_norm_g, kv_norm_b, W_u_kv, b_u_kv, W_o, b_o):
        import jax, jax.numpy as jnp
        import numpy as np
        D_MODEL = 256
        N_HEADS = 16
        D_HEAD = D_MODEL // N_HEADS
        D_Q = D_MODEL // 3
        D_KV = D_MODEL // 2
        D_QK_N = D_HEAD // 2
        D_QK_R = D_HEAD // 2
        EPS = 1e-05

        def _layernorm(x, g, b):
            mu = jnp.mean(x, axis=-1, keepdims=True)
            var = jnp.var(x, axis=-1, keepdims=True)
            return (x - mu) * jax.lax.rsqrt(var + EPS) * g + b

        def _rotary(x):
            d = x.shape[-1]
            inv_freq = (1.0 / 10000.0) ** (jnp.arange(0, d, 2, dtype=jnp.float32) / d)
            t = jnp.arange(x.shape[1], dtype=jnp.float32)
            freqs = t[:, None] * inv_freq[None, :]
            cos = jnp.cos(freqs)[None, :, None, :]
            sin = jnp.sin(freqs)[None, :, None, :]
            x1, x2 = jnp.split(x, 2, axis=3)
            return jnp.concatenate([x1 * cos + x2 * sin, -x1 * sin + x2 * cos], axis=3)
        B, T, C = x.shape
        H, dh, dqn, dqr, dkv = (N_HEADS, D_HEAD, D_QK_N, D_QK_R, D_KV)
        c_q = _layernorm(x @ W_d_q.T + b_d_q, q_norm_g, q_norm_b)
        q = (c_q @ W_u_q.T + b_u_q).reshape(B, T, H, dh).transpose(0, 2, 1, 3)
        q_n, q_r = (q[..., :dqn], q[..., dqn:])
        q_r = _rotary(q_r)
        c_kv = x @ W_d_kv.T + b_d_kv
        kv_n = _layernorm(c_kv[..., :dkv], kv_norm_g, kv_norm_b)
        k_r = c_kv[..., dkv:]
        kv = (kv_n @ W_u_kv.T + b_u_kv).reshape(B, T, H, dh + dqn).transpose(0, 2, 1, 3)
        k_n, v = (kv[..., :dqn], kv[..., dqn:])
        k_r = k_r.reshape(B, T, 1, dqr).transpose(0, 2, 1, 3)
        k_r = _rotary(k_r)
        k_r = jnp.broadcast_to(k_r, (B, H, T, dqr))
        q_full = jnp.concatenate([q_n, q_r], axis=-1)
        k_full = jnp.concatenate([k_n, k_r], axis=-1)
        scale = 1.0 / np.sqrt(dh)
        scores = jnp.einsum('bhqd,bhkd->bhqk', q_full, k_full) * scale
        causal = jnp.tril(jnp.ones((T, T), dtype=bool))
        scores = jnp.where(causal[None, None], scores, -jnp.inf)
        probs = jax.nn.softmax(scores, axis=-1)
        y = jnp.einsum('bhqk,bhkd->bhqd', probs, v)
        y = y.transpose(0, 2, 1, 3).reshape(B, T, C)
        return y @ W_o.T + b_o

    def _L0_ffn_ref(x, w_gate, w_up, w_down, s_gate, s_up, s_down):
        import jax, jax.numpy as jnp
        import numpy as np
        HIDDEN = 256
        INTER = 1024
        B, S = (4, 128)

        def _qmatmul(x, w_int8, scale):
            y = jnp.einsum('bsh,ho->bso', x, w_int8.astype(x.dtype))
            return y * scale
        gate = jax.nn.silu(_qmatmul(x, w_gate, s_gate))
        up = _qmatmul(x, w_up, s_up)
        fuse = gate * up
        return _qmatmul(fuse, w_down, s_down)

    def _L1_attn_ref(x, w_qkv, b_qkv, w_out, b_out):
        import jax, jax.numpy as jnp
        import numpy as np
        import math
        D_MODEL = 256
        NUM_HEADS = 16
        HEAD_DIM = D_MODEL // NUM_HEADS
        B, S, D = x.shape
        H, Hd = (NUM_HEADS, HEAD_DIM)
        qkv = jnp.einsum('bsd,ed->bse', x, w_qkv) + b_qkv
        qkv = qkv.reshape(B, S, 3, H, Hd)
        q = jnp.transpose(qkv[:, :, 0], (0, 2, 1, 3))
        k = jnp.transpose(qkv[:, :, 1], (0, 2, 1, 3))
        v = jnp.transpose(qkv[:, :, 2], (0, 2, 1, 3))
        scores = jnp.einsum('bhqd,bhkd->bhqk', q, k) / math.sqrt(Hd)
        causal = jnp.triu(jnp.full((S, S), -jnp.inf, dtype=scores.dtype), k=1)
        scores = scores + causal[None, None]
        attn = jax.nn.softmax(scores, axis=-1)
        out = jnp.einsum('bhqk,bhkd->bhqd', attn, v)
        out = jnp.transpose(out, (0, 2, 1, 3)).reshape(B, S, D)
        return jnp.einsum('bsd,ed->bse', out, w_out) + b_out

    def _L1_ffn_ref(x, w_gate, w_up, w_down, s_gate, s_up, s_down):
        import jax, jax.numpy as jnp
        import numpy as np
        HIDDEN = 256
        INTER = 1024
        B, S = (4, 128)

        def _qmatmul(x, w_int8, scale):
            y = jnp.einsum('bsh,ho->bso', x, w_int8.astype(x.dtype))
            return y * scale
        gate = jax.nn.silu(_qmatmul(x, w_gate, s_gate))
        up = _qmatmul(x, w_up, s_up)
        fuse = gate * up
        return _qmatmul(fuse, w_down, s_down)
    x = L0_attn_x
    x = x + _layernorm(_L0_attn_ref(_layernorm(x, axis=-1), L0_attn_W_d_q, L0_attn_b_d_q, L0_attn_q_norm_g, L0_attn_q_norm_b, L0_attn_W_u_q, L0_attn_b_u_q, L0_attn_W_d_kv, L0_attn_b_d_kv, L0_attn_kv_norm_g, L0_attn_kv_norm_b, L0_attn_W_u_kv, L0_attn_b_u_kv, L0_attn_W_o, L0_attn_b_o), axis=-1)
    x = x + _layernorm(_L0_ffn_ref(_layernorm(x, axis=-1), L0_ffn_w_gate, L0_ffn_w_up, L0_ffn_w_down, L0_ffn_s_gate, L0_ffn_s_up, L0_ffn_s_down), axis=-1)
    x = x + _layernorm(_L1_attn_ref(_layernorm(x, axis=-1), L1_attn_w_qkv, L1_attn_b_qkv, L1_attn_w_out, L1_attn_b_out), axis=-1)
    x = x + _layernorm(_L1_ffn_ref(_layernorm(x, axis=-1), L1_ffn_w_gate, L1_ffn_w_up, L1_ffn_w_down, L1_ffn_s_gate, L1_ffn_s_up, L1_ffn_s_down), axis=-1)
    return x

_drawn_inputs = setup_inputs


def setup_inputs(seed=0):
    import zlib

    import numpy as np

    out = dict(_drawn_inputs(seed))
    spreads = {'L0_attn_b_d_q': (0.0, 2.0),
     'L0_attn_q_norm_g': (1.0, 0.6),
     'L0_attn_q_norm_b': (0.0, 2.0),
     'L0_attn_b_u_q': (0.0, 2.0),
     'L0_attn_b_d_kv': (0.0, 0.1),
     'L0_attn_kv_norm_g': (1.0, 0.2),
     'L0_attn_kv_norm_b': (0.0, 0.1),
     'L0_attn_b_u_kv': (0.0, 0.1),
     'L0_attn_b_o': (0.0, 0.1)}
    factors = {'L0_attn_W_d_q': 8.0, 'L0_attn_W_u_q': 8.0, 'L1_attn_b_qkv': 6.576, 'L1_attn_b_out': 7.826}
    for name, (base, spread) in spreads.items():
        noise = np.random.default_rng([zlib.crc32(name.encode()), seed]).standard_normal(out[name].shape)
        drawn = base * np.exp(spread * noise) if base else spread * noise
        out[name] = jnp.asarray(drawn.astype(out[name].dtype))
    for name, factor in factors.items():
        out[name] = (out[name] * factor).astype(out[name].dtype)
    return out
```

```python
from contextlib import ExitStack
from collections import namedtuple

import numpy as np

import concourse.bass as bass
from concourse import mybir

ALU = mybir.AluOpType
ACT = mybir.ActivationFunctionType
AX = mybir.AxisListType
F32 = mybir.dt.float32
BF16 = mybir.dt.bfloat16
F16 = mybir.dt.float16
I8 = mybir.dt.int8

P = 128
T = 2048
C = 256
NT = T // P
KC = C // P
H = 16
DH = C // H
DQ = C // 3
DKV = C // 2
DN = DH // 2
DR = DH // 2
INTER = 1024
NI = INTER // P
EPS = 1e-5
CH = 512
NCH = T // CH
TPC = CH // P
HG = 4
NG = H // HG
PAIRS = NG // 2
Q_PARTS = (0, 0, 1, 1, 0, 2)
K_PARTS = (0, 1, 0, 1, 2, 0)
NSTACK = DH * len(Q_PARTS)
NM = 3
KROWS = NSTACK + NM
VW = DH + 1
MASKED = -3.0e38
SCALE = 1.0 / DH ** 0.5

COLS = {"q_g": 0, "q_b": 1, "kv_g": 2, "kv_b": 3, "b_uq": 4, "b_uq_swap": 6, "b_kn": 8, "b_kr": 9,
        "b_qk1": 10, "s_gate": (14, 30), "s_up": (22, 38),
        "cos": 46, "sin": 48}
NCOLS = 50
ROWS = {"b_down": (0, DQ + DKV), "b_v": ((213, 256), (725, 256)), "b_o": ((469, 256), (981, 256)),
        "s_down": ((1237, 256), (1493, 256)), "cos": (1749, 256), "sin": (2005, 256)}
NROWS = 2261

Step = namedtuple("Step", "kind n buf Q h r c kt off first last hp ring k j sel", defaults=(None,) * 14)


def plan_pair():
    steps = [(0, 0), (0, 1), (0, 2), (0, 3), (1, 3), (1, 2), (1, 1), (1, 0)]
    s_units = [(n, h, r, c) for n, (_, Q) in enumerate(steps) for h in range(HG) for r in range(TPC)
               for c in range(Q + 1)]
    s_count = [0] * len(steps)
    for u in s_units:
        s_count[u[0]] += 1
    kts = [list(range(TPC * Q, TPC * Q + TPC)) + list(range(TPC * Q)) for _, Q in steps]
    order = []
    pe = dve = act = pool = 0.0
    ring_free = [0.0] * 3
    m_parts = {}
    m_rows = {}
    pair_free = [0.0] * 2
    slot_free = [0.0] * 3
    evac = {}
    exp_end = {}
    v_free = 0.0
    ring = k = j_t = j_pv = sel = 0
    si = mt = yt = 0
    t_list = [(n, i, kt, hp) for n in range(len(steps)) for i, kt in enumerate(kts[n]) for hp in range(2)]
    pv_list = [(n, i, kt) for n in range(len(steps)) for i, kt in enumerate(kts[n])]
    ti = pi = 0
    while yt < len(steps):
        cand = []
        if mt < len(steps) and mt in m_parts:
            cand.append((0, max(m_parts[mt], ring_free[ring % 3]), "MT"))
        if yt in evac:
            cand.append((1, max(evac[yt], ring_free[ring % 3]), "YT"))
        if si < len(s_units) and s_units[si][0] < mt + 2:
            cand.append((2, ring_free[ring % 3], "S"))
        if pi < len(pv_list) and pi in exp_end:
            n, i, kt = pv_list[pi]
            ready = exp_end[pi]
            if i == 0:
                ready = max(ready, v_free)
            if i > 0 or n == 0 or n - 1 in evac:
                cand.append((3, ready, "PV"))
        if ti < len(t_list):
            n, i, kt, hp = t_list[ti]
            if n in m_rows and ti // 2 < pi + 3:
                cand.append((4, max(m_rows[n], pair_free[k % 2]), "T"))
        ready_now = [x for x in cand if x[1] <= pe + 1]
        prio, ready, kind = min(ready_now) if ready_now else min(cand, key=lambda x: (x[1], x[0]))
        pe = max(pe, ready)
        if kind == "S":
            n, h, r, c = s_units[si]
            buf, Q = steps[n]
            cols = CH if c < Q else P * (r + 1)
            pe += cols / 2.4 + (53 if c == Q else 0)
            dve = max(dve, pe + 100) + cols / 0.96 + 70
            ring_free[ring % 3] = dve
            si += 1
            last = si == len(s_units) or s_units[si][0] != n
            order.append(Step("S", n, buf, Q, h=h, r=r, c=c, last=last, ring=ring))
            ring += 1
            if last:
                pool = max(pool, dve + 200) + 2500
                dve += 150
                m_parts[n] = pool + 200
        elif kind == "MT":
            buf, Q = steps[mt]
            pe += 100
            dve = max(dve, pe + 100) + 200
            ring_free[ring % 3] = dve
            order.append(Step("MT", mt, buf, Q, ring=ring))
            ring += 1
            m_rows[mt] = dve + 3000
            mt += 1
        elif kind == "YT":
            buf, Q = steps[yt]
            pe += 250
            dve = max(dve, pe + 100) + 600
            ring_free[ring % 3] = dve
            order.append(Step("YT", yt, buf, Q, ring=ring))
            ring += 1
            yt += 1
        elif kind == "T":
            n, i, kt, hp = t_list[ti]
            buf, Q = steps[n]
            off = P * (kt - TPC * Q) if kt >= TPC * Q else 0
            pe += 2 * (CH - off) / 2.4
            act = max(act, pe + 100) + 2 * (CH - off) / 1.2 + 60
            pair_free[k % 2] = act
            diag = kt >= TPC * Q
            order.append(Step("T", n, buf, Q, kt=kt, off=off, hp=hp, k=k, j=ti // 2, first=diag,
                              last=i == len(kts[n]) - 1 and hp == 1, sel=sel))
            k += 1
            if hp == 1:
                exp_end[ti // 2] = act + 200
                if diag:
                    pool = max(pool, act) + 700
                    exp_end[ti // 2] = pool + 100
                    sel += 1
            ti += 1
        else:
            n, i, kt = pv_list[pi]
            buf, Q = steps[n]
            off = P * (kt - TPC * Q) if kt >= TPC * Q else 0
            pe += 4 * (CH - off) / 2.4
            last = i == len(kts[n]) - 1
            diag_before = sum(1 for m, _, q in pv_list[:pi + 1] if q >= TPC * steps[m][1])
            order.append(Step("PV", n, buf, Q, kt=kt, off=off, first=i == 0, last=last, j=pi,
                              sel=diag_before if kt >= TPC * Q else None))
            if last:
                act = max(act, pe + 150) + 550
                v_free = evac[n] = act + 100
            pi += 1
    return steps, order


def build_program(nc, D, out):
    STEPS, ORDER = plan_pair()
    NSTEP = len(STEPS)
    RING_N = sum(1 for o in ORDER if o.ring is not None)
    T_N = sum(1 for o in ORDER if o.kind == "T")
    PV_N = sum(1 for o in ORDER if o.kind == "PV")
    SEL_N = max(o.sel for o in ORDER if o.kind == "PV" and o.sel is not None)
    S_LAST = {o.n: o.ring for o in ORDER if o.kind == "S" and o.last}
    MT_RING = {o.n: o.ring for o in ORDER if o.kind == "MT"}
    YT_RING = {o.n: o.ring for o in ORDER if o.kind == "YT"}
    PV_LAST = {o.n: o.j for o in ORDER if o.kind == "PV" and o.last}
    T_LAST_OF_BUF = [max(o.k for o in ORDER if o.kind == "T" and o.buf == b) for b in range(2)]

    with ExitStack() as ctx:
        def sb(name, shape, dt):
            return ctx.enter_context(nc.sbuf_tensor(name, shape, dt))

        def sem(name):
            return ctx.enter_context(nc.semaphore(name))

        X = sb("X", [P, NT, C], F32)
        region_a = sb("region_a", [P, NT * C], F32)
        region_v = sb("region_v", [P, NT * C], F32)
        region_vst = sb("region_vst", [P, 2 * NT * HG * VW], F32)
        region_p = sb("region_p", [P, 3 * HG * CH], F32)
        q_stack = sb("q_stack", [P, 2, NCH, HG, CH], BF16)
        k_stack = sb("k_stack", [P, 2, HG, T], BF16)
        w_attn = sb("w_attn", [P, 2048], F32)
        w_ffn = sb("w_ffn", [P, 3 * KC * INTER], BF16)
        w_raw = sb("w_raw", [P, 3 * KC * INTER], I8)
        cols = sb("cols", [P, NCOLS], F32)
        rows = sb("rows", [P, NROWS], F32)
        ident = sb("ident", [P, P], F32)
        ident_bf = sb("ident_bf", [P, P], BF16)
        causal = sb("causal", [P, P], BF16)
        val = sb("val", [P, 2, CH], F32)
        rem = sb("rem", [P, 2, CH], F32)
        parts = sb("parts", [P, 3, 3, CH], BF16)
        y_chunk = sb("y_chunk", [P, 2, CH], F32)
        m_tile = sb("m_tile", [P, 2, HG * TPC, NCH], F32)
        neg_max = sb("neg_max", [P, 2, HG * TPC], F32)
        m_rem = sb("m_rem", [P, 2, HG * TPC], F32)
        m_parts = sb("m_parts", [P, 2, P], BF16)
        m_rows = sb("m_rows", [NM * HG * TPC, 2, P], BF16)
        recip = sb("recip", [P, TPC, HG], F32)
        stats = sb("stats", [P, NT, 2, 6], F32)
        mv = sb("mv", [P, NT, 2, 2], F32)
        std = sb("std", [P, NT, 2], F32)
        rstd = sb("rstd", [P, NT, 2], F32)
        eps = sb("eps", [P, 1], F32)
        ps = ctx.enter_context(nc.psum_tensor("ps", [P, 8, 512], F32))

        XT = region_a[:].rearrange("p (k t) -> p k t", k=KC)
        Y = region_a[:].rearrange("p (i c) -> p i c", i=NT)
        x16 = region_a[:].bitcast(F16).rearrange("p (s k t) -> p s k t", s=2, k=KC)
        V = region_v[:].rearrange("p (i c) -> p i c", i=NT)
        v_stage = region_vst[:].rearrange("p (b i h w) -> p b i h w", b=2, i=NT, h=HG)
        probs = region_p[:].rearrange("p (s h q) -> p s h q", s=3, h=HG)
        A = region_p[:, 0:NT * C].rearrange("p (i c) -> p i c", i=NT)
        c_down = region_p[:, 0:NT * (DQ + DKV)].rearrange("p (i c) -> p i c", i=NT)
        q_flat = q_stack[:].rearrange("p b q h t -> p (b q h t)").bitcast(F32)
        cq_t, ckv_t = (q_flat[:, i * T:(i + 1) * T] for i in range(2))
        y_t = q_flat[:, 0:2 * CH].rearrange("p (b k t) -> p b k t", b=2, k=KC * 2)
        gate_r = region_v[:, 0:2 * CH].rearrange("p (s t) -> p s t", s=2)
        fuse_r = region_v[:, 2 * CH:5 * CH].rearrange("p (s t) -> p s t", s=3)
        frem_r = region_v[:, 5 * CH:8 * CH].rearrange("p (s t) -> p s t", s=3)
        flo_r = region_vst[:, 0:3 * CH // 2].bitcast(BF16).rearrange("p (s t) -> p s t", s=3)
        fuse_hi = fuse_r.bitcast(BF16).rearrange("p s (t two) -> p s t two", two=2)[:, :, :, 1]
        frem_hi = frem_r.bitcast(BF16).rearrange("p s (t two) -> p s t two", two=2)[:, :, :, 1]
        w_down = w_attn[:, 0:KC * 213].rearrange("p (k c) -> p k c", k=KC)
        w_kr = w_attn[:, 426:426 + KC * DR].rearrange("p (k c) -> p k c", k=KC)
        w_uq = w_attn[0:DQ, 506:762]
        w_uq_swap = w_attn[0:DQ, 762:1018]
        w_kn = w_attn[:, 1018:1146]
        w_v0 = w_attn[:, 1146:1402]
        w_qkv = w_attn[:, 0:KC * 3 * C].rearrange("p (k c) -> p k c", k=KC)
        w_o = w_attn[:, 1536:2048].rearrange("p (k c) -> p k c", k=KC)
        w_gate, w_up = (w_ffn[:, i * KC * INTER:(i + 1) * KC * INTER].rearrange("p (k c) -> p k c", k=KC)
                        for i in range(2))
        w_dn = w_ffn[:, 2 * KC * INTER:].rearrange("p (k c) -> p k c", k=NI)
        psT = ps[:, 0:4, :].rearrange("p (b h) q -> p b h q", b=2)
        RING0, PV_BANK = 4, 7

        def col(name, width=1, n=P, layer=None, at=0):
            c = COLS[name] if layer is None else COLS[name][layer]
            return cols[0:n, c + at:c + at + width]

        def row(name, layer=None):
            a, n = ROWS[name] if layer is None else ROWS[name][layer]
            return rows[:, a:a + n]

        consts_in = sem("consts_in")
        x_in = [sem(f"x_in{i}") for i in range(4)]
        w_in = [sem(f"w_in{L}") for L in range(2)]
        wraw_in = [sem(f"wraw_in{L}") for L in range(2)]
        wffn_done = [sem(f"wffn_done{L}") for L in range(2)]
        setup_done = sem("setup_done")
        ones_done = sem("ones_done")
        out_stored = sem("out_stored")

        def Sems(stage, *names):
            return namedtuple(stage, names)(*[sem(f"{stage}_{n}") for n in names])

        TURN_IN = ("stats_done", "std_done", "rstd_done", "normed", "added")
        TURN_OUT = ("stats2", "var2", "std2", "rstd2", "xhat", "tpose", "moved_a", "moved_v")
        turn = [Sems(f"turn{k}", *(TURN_IN if k > 0 else ()), *(TURN_OUT if k < 4 else ())) for k in range(5)]
        SPLIT = ("u_ps", "val", "hi", "rem", "mid", "lo", "v_ps", "v_sb")
        proj = [Sems("proj0", *SPLIT, "rot", "down_ps", "down_sb", "stat", "var", "std", "rstd", "z", "zt_ps", "zq_sb",
                     "zkv_sb"), Sems("proj1", *SPLIT)]
        parts_stored = [[sem(f"parts_stored{L}{b}") for b in range(3)] for L in range(2)]
        stack_in = [[sem(f"stack{L}{b}") for b in range(2)] for L in range(2)]
        s = Sems("att", "ring_filled", "ring_free", "negmax", "mparts", "t_filled", "exp_done", "selected",
                 "pv_done", "y_evac", "rcp", "v_staged", "v_ones")
        mrows_in = [sem(f"mrows_in{i}") for i in range(2)]
        MROWS_N = 16 * NM * (NSTEP // 2)
        oproj = [Sems(f"oproj{L}", "yt_ps", "yt_sb", "o_ps", "o_sb", "st") for L in range(2)]
        ffn = [Sems(f"ffn{L}", "gu_ps", "gate", "fuse", "rem", "lo", "down", "evac", "st") for L in range(2)]

        UNITS = [
            [("kr", 0, c) for c in range(NCH)] + [("q", m, c) for m in range(2) for c in range(NCH)]
            + [("kn", 0, c) for c in range(NCH)],
            [("qk", m, c) for m in range(4) for c in range(NCH)],
        ]
        NU = 16
        VU = NT // 2
        part_dram = {"q": D["q_parts"], "kn": D["kn_parts"], "kr": D["kr_parts"]}

        def unit_rows(L, u):
            kind, m, c = UNITS[L][u]
            return DR if kind == "kr" else P

        def unit_dram(L, u):
            kind, m, c = UNITS[L][u]
            if kind == "qk":
                t, m = (D["q_parts"], m) if m < 2 else (D["k_parts"], m - 2)
            else:
                t = part_dram[kind]
            n = unit_rows(L, u)
            return t[:, m * P:m * P + n, c * CH:(c + 1) * CH].rearrange("s r t -> r s t")

        block = ctx.enter_context(nc.Block())

        @block.sync
        def _(sp):
            xin = D["x"].rearrange("(i p) c -> p i c", p=P)
            for g in range(4):
                sp.dma_start(X[:, 4 * g:4 * g + 4, :], xin[:, 4 * g:4 * g + 4, :]).then_inc(x_in[g], 16)

            for L in range(2):
                for u in range(NU):
                    sp.wait_ge(proj[L].lo, u + 1)
                    n = unit_rows(L, u)
                    sp.dma_start(unit_dram(L, u), parts[0:n, u % 3, :, :]).then_inc(parts_stored[L][u % 3], 16)
                for b in range(3):
                    sp.wait_ge(parts_stored[L][b], 16 * ((NU - b + 2) // 3))

                def load_stack(g):
                    b = g % 2
                    loaded = stack_in[L][b]
                    for k, part in enumerate(Q_PARTS):
                        src = D["q_parts"][part, g * HG * DH:(g + 1) * HG * DH, :]
                        for q in range(NCH):
                            sp.dma_start(q_stack[DH * k:DH * (k + 1), b, q, :, :],
                                         src[:, q * CH:(q + 1) * CH].rearrange("(h d) t -> d h t", h=HG)).then_inc(loaded, 16)
                    for k, part in enumerate(K_PARTS):
                        if L == 0:
                            src = D["kn_parts"][part, g * HG * DN:(g + 1) * HG * DN, :]
                            sp.dma_start(k_stack[DH * k:DH * k + DN, b, :, :],
                                         src.rearrange("(h d) t -> d h t", h=HG)).then_inc(loaded, 16)
                            sp.dma_start(k_stack[DH * k + DN:DH * (k + 1), b, :, :],
                                         D["kr_parts"][part, :, :].rearrange("d (o t) -> d o t", o=1)
                                         .broadcast_to([DR, HG, T])).then_inc(loaded, 16)
                        else:
                            src = D["k_parts"][part, g * HG * DH:(g + 1) * HG * DH, :]
                            sp.dma_start(k_stack[DH * k:DH * (k + 1), b, :, :],
                                         src.rearrange("(h d) t -> d h t", h=HG)).then_inc(loaded, 16)

                if L == 0:
                    sp.wait_ge(proj[L].v_ps, VU)
                load_stack(0)
                load_stack(1)
                for it in range(PAIRS * L, PAIRS * (L + 1)):
                    for o in ORDER:
                        if o.kind == "MT":
                            sp.wait_ge(s.ring_free, it * RING_N + o.ring + 1)
                            for m in range(NM):
                                dst = q_stack[NSTACK + m:NSTACK + m + 1, o.buf, o.Q, :, :].rearrange(
                                    "o h (r t) -> o (h r) t", r=TPC)
                                src = m_rows[m * HG * TPC:(m + 1) * HG * TPC, o.n % 2, :]
                                sp.dma_start(dst, src).then_inc(mrows_in[o.n % 2], 16)
                        if o.kind == "T" and it + 1 < PAIRS * (L + 1) and o.k in T_LAST_OF_BUF:
                            sp.wait_ge(s.t_filled, it * T_N + o.k + 1)
                            load_stack(2 * (it + 1 - PAIRS * L) + o.buf)

            for g in range(4):
                sp.wait_ge(turn[4].added, 4 * g + 4)
                sp.dma_start(out.rearrange("(i p) c -> p i c", p=P)[:, 4 * g:4 * g + 4, :],
                             X[:, 4 * g:4 * g + 4, :]).then_inc(out_stored, 16)
            sp.wait_ge(out_stored, 64)

        @block.gpsimd
        def _(pool):
            def load_weights(L):
                if L == 0:
                    pool.dma_start(w_down, D["w_down"]).then_inc(w_in[0], 16)
                    pool.dma_start(w_kr, D["w_kr"]).then_inc(w_in[0], 16)
                    pool.dma_start(w_uq, D["w_uq"]).then_inc(w_in[0], 16)
                    pool.dma_start(w_uq_swap, D["w_uq_swap"]).then_inc(w_in[0], 16)
                    pool.dma_start(w_kn, D["w_kn"]).then_inc(w_in[0], 16)
                    pool.dma_start(w_v0, D["w_v0"]).then_inc(w_in[0], 16)
                else:
                    pool.wait_ge(oproj[0].o_ps, NT // 2)
                    pool.dma_start(w_qkv, D["w_qkv"]).then_inc(w_in[1], 16)
                pool.dma_start(w_o, D["w_o"][L]).then_inc(w_in[L], 16)

            def load_ffn(L):
                if L == 1:
                    pool.wait_ge(wffn_done[0], 3)
                raw = w_raw[:].bitcast(mybir.dt.int32).rearrange("p (s c) -> p s c", s=3)
                for s, name in enumerate(("w_gate", "w_up", "w_dn")):
                    pool.dma_start(raw[:, s, :], D[name][L]).then_inc(wraw_in[L], 16)

            pool.dma_start(cols[:], D["cols"]).then_inc(consts_in, 16)
            pool.dma_start(rows[:], D["rows"].broadcast_to([P, NROWS])).then_inc(consts_in, 16)
            pool.dma_start(ident[:], D["ident"]).then_inc(consts_in, 16)
            pool.dma_start(ident_bf[:], D["ident_bf"]).then_inc(consts_in, 16)
            pool.dma_start(causal[:], D["causal"]).then_inc(consts_in, 16)
            load_weights(0)
            load_ffn(0)
            nc.gpsimd.memset(k_stack[NSTACK:KROWS, :, :, :], 1.0).then_inc(ones_done, 1)
            pool.wait_ge(ones_done, 1)

            def split_lo(L, u):
                n = unit_rows(L, u)
                pool.wait_ge(proj[L].mid, u + 1)
                nc.gpsimd.tensor_tensor(parts[0:n, u % 3, 2, :], rem[0:n, u % 2, :], parts[0:n, u % 3, 1, :],
                                        ALU.subtract).then_inc(proj[L].lo, 1)

            def add_residual(k, i):
                pool.wait_ge(turn[k].normed, i + 1)
                nc.gpsimd.tensor_tensor(X[:, i, :], X[:, i, :], A[:, i, :], ALU.add).then_inc(turn[k].added, 1)

            for L in range(2):
                for u in range(NU):
                    split_lo(L, u)
                pool.wait_ge(proj[L].v_sb, VU)
                nc.gpsimd.memset(v_stage[:, :, :, :, DH:VW], 1.0).then_inc(s.v_ones, 1)
                for it in range(PAIRS * L, PAIRS * (L + 1)):
                    for b in range(2):
                        if it > 0:
                            pool.wait_ge(s.pv_done, it * PV_N)
                        src = V[:, :, bass.ds((it - PAIRS * L) * (2 * HG * DH) + b * HG * DH, HG * DH)]
                        nc.gpsimd.tensor_copy(v_stage[:, b, :, :, 0:DH], src.rearrange("p i (h d) -> p i h d", h=HG)
                                              ).then_inc(s.v_staged, 1)
                    for o in ORDER:
                        if o.kind == "S" and o.last:
                            nm, mr = neg_max[:, o.n % 2, :], m_rem[:, o.n % 2, :]
                            mp = m_parts[:, o.n % 2, 0:NM * HG * TPC].rearrange("p (s m) -> p s m", s=NM)
                            c0 = it * (4 * NSTEP) + 4 * o.n
                            pool.wait_ge(s.negmax, it * NSTEP + o.n + 1)
                            if o.n >= 2:
                                pool.wait_ge(s.ring_filled, it * RING_N + MT_RING[o.n - 2] + 1)
                            elif it > 0:
                                pool.wait_ge(s.ring_filled, it * RING_N)
                            nc.gpsimd.tensor_copy(mp[:, 0, :], nm).then_inc(s.mparts, 1)
                            pool.wait_ge(s.mparts, c0 + 1)
                            nc.gpsimd.tensor_tensor(mr, nm, mp[:, 0, :], ALU.subtract).then_inc(s.mparts, 1)
                            pool.wait_ge(s.mparts, c0 + 2)
                            nc.gpsimd.tensor_copy(mp[:, 1, :], mr).then_inc(s.mparts, 1)
                            pool.wait_ge(s.mparts, c0 + 3)
                            nc.gpsimd.tensor_tensor(mp[:, 2, :], mr, mp[:, 1, :], ALU.subtract).then_inc(s.mparts, 1)
                        if o.kind == "T" and o.first and o.hp == 1:
                            pool.wait_ge(s.exp_done, it * T_N + o.k + 1)
                            blk = probs[:, o.j % 3, :, o.off:o.off + P]
                            nc.gpsimd.affine_select(out=blk, in_=blk, compare_op=ALU.is_ge, fill=0.0, base=0,
                                                    pattern=[[0, HG], [1, P]], channel_multiplier=-1
                                                    ).then_inc(s.selected, 1)
                if L == 0:
                    load_weights(1)
                for i in range(NT):
                    add_residual(1 + 2 * L, i)
                for u in range(NCH * NI):
                    pool.wait_ge(ffn[L].rem, u + 1)
                    if u >= 3:
                        pool.wait_ge(ffn[L].down, u - 2)
                    nc.gpsimd.tensor_tensor(flo_r[:, u % 3, :], frem_r[:, u % 3, :], frem_hi[:, u % 3, :],
                                            ALU.subtract).then_inc(ffn[L].lo, 1)
                if L == 0:
                    load_ffn(1)
                for i in range(NT):
                    add_residual(2 + 2 * L, i)

        @block.scalar
        def _(act):
            def turn_scalar(k):
                tn = turn[k]
                if k > 0:
                    act.wait_ge(tn.stats_done, NT)
                    nc.scalar.activation(std[:, :, 0], mv[:, :, 0, 1], ACT.Sqrt, bias=eps[:]).then_inc(tn.std_done, 1)
                if k == 4:
                    return
                act.wait_ge(tn.stats2, NT)
                nc.scalar.activation(std[:, :, 1], mv[:, :, 1, 1], ACT.Sqrt, bias=eps[:]).then_inc(tn.std2, 1)
                for u in range(NT // 2):
                    act.wait_ge(tn.tpose, u + 1)
                    src = ps[:, u % 4, :].rearrange("p (k t) -> p k t", k=KC)
                    if k % 2 == 0:
                        nc.scalar.copy(XT[:, :, u * 2 * P:(u + 1) * 2 * P], src).then_inc(tn.moved_a, 1)
                    else:
                        nc.scalar.copy(x16[:, 0, :, u * 2 * P:(u + 1) * 2 * P], src).then_inc(tn.moved_a, 1)

            def convert_ffn(L):
                act.wait_ge(wraw_in[L], 48)
                if L == 1:
                    act.wait_ge(ffn[0].down, NCH * NI)
                n = KC * INTER
                for k in range(3):
                    nc.scalar.copy(w_ffn[:, k * n:(k + 1) * n], w_raw[:, k * n:(k + 1) * n]).then_inc(wffn_done[L], 1)

            def split_hi(L, u):
                n = unit_rows(L, u)
                act.wait_ge(proj[L].val, u + 1)
                if u >= 3:
                    act.wait_ge(parts_stored[L][u % 3], 16 * (u // 3))
                nc.scalar.copy(parts[0:n, u % 3, 0, :], val[0:n, u % 2, :]).then_inc(proj[L].hi, 1)

            def split_mid(L, u):
                n = unit_rows(L, u)
                act.wait_ge(proj[L].rem, u + 1)
                nc.scalar.copy(parts[0:n, u % 3, 1, :], rem[0:n, u % 2, :]).then_inc(proj[L].mid, 1)

            act.wait_ge(setup_done, 3)
            for L in range(2):
                turn_scalar(2 * L)
                convert_ffn(L)
                if L == 0:
                    p = proj[0]
                    act.wait_ge(p.stat, 2 * NT)
                    nc.scalar.activation(std[:], mv[:, :, :, 1], ACT.Sqrt, bias=eps[:]).then_inc(p.std, 1)
                    for g in range(NCH):
                        act.wait_ge(p.zt_ps, g + 1)
                        nc.scalar.activation(cq_t[0:DQ, g * CH:(g + 1) * CH], ps[0:DQ, 4 + 2 * (g % 2), :], ACT.Identity,
                                             scale=col("q_g", n=DQ), bias=col("q_b", n=DQ)).then_inc(p.zq_sb, 1)
                for u in range(NU):
                    split_hi(L, u)
                    if u > 0:
                        split_mid(L, u - 1)
                split_mid(L, NU - 1)

                with act.Fori(PAIRS * L, PAIRS * (L + 1)) as it:
                    for o in ORDER:
                        if o.kind == "T":
                            act.wait_ge(s.t_filled, it * T_N + o.k + 1)
                            if o.j >= 3:
                                act.wait_ge(s.pv_done, it * PV_N + o.j - 2)
                            nc.scalar.activation(probs[:, o.j % 3, 2 * o.hp:2 * o.hp + 2, o.off:CH],
                                                 psT[:, o.k % 2, :, o.off:CH], ACT.Exp, scale=SCALE
                                                 ).then_inc(s.exp_done, 1)
                        if o.kind == "PV" and o.last:
                            act.wait_ge(s.pv_done, it * PV_N + o.j + 1)
                            if o.n >= 2:
                                act.wait_ge(s.ring_filled, it * RING_N + YT_RING[o.n - 2] + 1)
                            nc.scalar.copy(y_chunk[:, o.n % 2, :], ps[:, PV_BANK, :]).then_inc(s.y_evac, 1)
                    act.wait_ge(s.pv_done, it * PV_N + PV_N)
                    act.wait_ge(s.ring_filled, it * RING_N + RING_N)

                for u in range(NT // 2):
                    act.wait_ge(oproj[L].yt_ps, u + 1)
                    if u >= 2:
                        act.wait_ge(oproj[L].o_ps, u - 1)
                    nc.scalar.copy(y_t[:, u % 2, :, :], ps[:, u % 2, :].rearrange("p (k t) -> p k t", t=P)
                                   ).then_inc(oproj[L].yt_sb, 1)
                turn_scalar(1 + 2 * L)
                f = ffn[L]
                for u in range(NCH * NI):
                    act.wait_ge(f.gu_ps, u + 1)
                    if u >= 2:
                        act.wait_ge(f.fuse, u - 1)
                    it_ = u % NI
                    nc.scalar.activation(gate_r[:, u % 2, :], ps[:, u % 2, :], ACT.Silu,
                                         scale=col("s_gate", layer=L, at=it_)).then_inc(f.gate, 1)
            turn_scalar(4)

        @block.vector
        def _(dve):
            def stats_of(src, i, which, after, done):
                nc.vector.bn_stats(stats[:, i, which, :], src).then_inc(after, 1)
                dve.wait_ge(after, i + 1)
                nc.vector.bn_aggr(mv[:, i, which, :], stats[:, i, which, :]).then_inc(done, 1)

            def turn_vector(k):
                tn = turn[k]
                if k > 0:
                    dve.wait_ge(tn.std_done, 1)
                    nc.vector.reciprocal(rstd[:, :, 0], std[:, :, 0]).then_inc(tn.rstd_done, 1)
                    dve.wait_ge(tn.rstd_done, 1)
                    for i in range(NT):
                        nc.vector.tensor_scalar(A[:, i, :], A[:, i, :], mv[:, i, 0, 0:1], rstd[:, i, 0:1], ALU.subtract,
                                                ALU.mult).then_inc(tn.normed, 1)
                if k == 4:
                    return
                for i in range(NT):
                    if k > 0:
                        dve.wait_ge(tn.added, i + 1)
                    else:
                        dve.wait_ge(x_in[i // 4], 16)
                    stats_of(X[:, i, :], i, 1, tn.var2, tn.stats2)
                dve.wait_ge(tn.std2, 1)
                nc.vector.reciprocal(rstd[:, :, 1], std[:, :, 1]).then_inc(tn.rstd2, 1)
                dve.wait_ge(tn.rstd2, 1)
                for i in range(NT):
                    nc.vector.tensor_scalar(A[:, i, :], X[:, i, :], mv[:, i, 1, 0:1], rstd[:, i, 1:2], ALU.subtract,
                                            ALU.mult).then_inc(tn.xhat, 1)
                if k % 2 == 1:
                    for u in range(NT // 2):
                        dve.wait_ge(tn.moved_a, u + 1)
                        sl = slice(u * 2 * P, (u + 1) * 2 * P)
                        nc.vector.tensor_tensor(x16[:, 1, :, sl], ps[:, u % 4, :].rearrange("p (k t) -> p k t", k=KC),
                                                x16[:, 0, :, sl], ALU.subtract).then_inc(tn.moved_v, 1)

            def unit_value(L, u):
                p = proj[L]
                kind, m, c = UNITS[L][u]
                n = unit_rows(L, u)
                dve.wait_ge(p.u_ps, u + 1)
                if u >= 2:
                    dve.wait_ge(p.rem, u - 1)
                dst = val[0:n, u % 2, :]
                b = 2 * (u % 2)
                bias = {"kr": col("b_kr", n=n), "q": col("b_uq", at=m), "kn": col("b_kn"),
                        "qk": col("b_qk1", at=m)}[kind]
                nc.vector.tensor_scalar(dst, ps[0:n, b, :], bias, None, ALU.add).then_inc(p.val, 1)

            def unit_rem(L, u):
                p = proj[L]
                n = unit_rows(L, u)
                dve.wait_ge(p.hi, u + 1)
                if u >= 2:
                    dve.wait_ge(p.lo, u - 1)
                nc.vector.tensor_tensor(rem[0:n, u % 2, :], val[0:n, u % 2, :], parts[0:n, u % 3, 0, :],
                                        ALU.subtract).then_inc(p.rem, 1)

            nc.vector.memset(m_parts[:], 0.0).then_inc(setup_done, 1)
            nc.vector.memset(eps[:], EPS).then_inc(setup_done, 1)
            nc.vector.memset(ps[:, PV_BANK, :], 0.0).then_inc(setup_done, 1)
            dve.wait_ge(consts_in, 80)
            for L in range(2):
                p = proj[L]
                if L == 0:
                    dve.wait_ge(w_in[0], 16 * 7)
                    for a, name in ((w_uq, "cos"), (w_uq_swap, "sin")):
                        nc.vector.tensor_tensor(a, a, row(name)[0:DQ, :], ALU.mult).then_inc(p.rot, 1)
                    for a, name in (("b_uq", "cos"), ("b_uq_swap", "sin")):
                        nc.vector.tensor_tensor(col(a, 2), col(a, 2), col(name, 2), ALU.mult).then_inc(p.rot, 1)
                    dve.wait_ge(p.rot, 4)
                    nc.vector.tensor_tensor(w_uq, w_uq, w_uq_swap, ALU.add).then_inc(p.rot, 1)
                    nc.vector.tensor_tensor(col("b_uq", 2), col("b_uq", 2), col("b_uq_swap", 2), ALU.add
                                            ).then_inc(p.rot, 1)
                    dve.wait_ge(p.rot, 6)
                turn_vector(2 * L)
                if L == 0:
                    for i in range(NT):
                        dve.wait_ge(p.down_ps, i + 1)
                        if i == 0:
                            dve.wait_ge(turn[0].tpose, NT // 2)
                        nc.vector.tensor_tensor(c_down[:, i, :], ps[:, 4 + i % 2, 0:DQ + DKV], row("b_down"),
                                                ALU.add).then_inc(p.down_sb, 1)
                        dve.wait_ge(p.down_sb, i + 1)
                        for w, cs in enumerate((slice(0, DQ), slice(DQ, DQ + DKV))):
                            nc.vector.bn_stats(stats[:, i, w, :], c_down[:, i, cs]).then_inc(p.var, 1)
                        dve.wait_ge(p.var, 2 * i + 2)
                        for w in range(2):
                            nc.vector.bn_aggr(mv[:, i, w, :], stats[:, i, w, :]).then_inc(p.stat, 1)
                    dve.wait_ge(p.std, 1)
                    nc.vector.reciprocal(rstd[:], std[:]).then_inc(p.rstd, 1)
                    dve.wait_ge(p.rstd, 1)
                    for i in range(NT):
                        for w, cs in enumerate((slice(0, DQ), slice(DQ, DQ + DKV))):
                            nc.vector.tensor_scalar(c_down[:, i, cs], c_down[:, i, cs], mv[:, i, w, 0:1],
                                                    rstd[:, i, w:w + 1], ALU.subtract, ALU.mult).then_inc(p.z, 1)
                    for g in range(NCH):
                        dve.wait_ge(p.zt_ps, g + 1)
                        nc.vector.tensor_scalar(ckv_t[:, g * CH:(g + 1) * CH], ps[:, 5 + 2 * (g % 2), :], col("kv_g"),
                                                col("kv_b"), ALU.mult, ALU.add).then_inc(p.zkv_sb, 1)
                for u in range(NU):
                    unit_value(L, u)
                    if u > 0:
                        unit_rem(L, u - 1)
                unit_rem(L, NU - 1)
                for u in range(VU):
                    dve.wait_ge(p.v_ps, u + 1)
                    for t in range(2):
                        ins = nc.vector.tensor_tensor(V[:, 2 * u + t, :], ps[:, 6 + u % 2, t * C:(t + 1) * C],
                                                      row("b_v", L), ALU.add)
                        if t == 1:
                            ins.then_inc(p.v_sb, 1)

                with dve.Fori(PAIRS * L, PAIRS * (L + 1)) as it:
                    base = it * RING_N
                    for o in ORDER:
                        if o.kind == "S":
                            n = CH if o.c < o.Q else P * (o.r + 1)
                            if o.h == o.r == o.c == 0 and o.n >= 2:
                                dve.wait_ge(s.negmax, it * NSTEP + o.n - 1)
                            dve.wait_ge(s.ring_filled, base + o.ring + 1)
                            nc.vector.tensor_reduce(m_tile[:, o.n % 2, o.h * TPC + o.r, o.c:o.c + 1],
                                                    ps[:, RING0 + o.ring % 3, 0:n], AX.X, ALU.max).then_inc(s.ring_free, 1)
                            if o.last:
                                dve.wait_ge(s.ring_free, base + o.ring + 1)
                                if o.n >= 2:
                                    dve.wait_ge(s.mparts, it * (4 * NSTEP) + 4 * (o.n - 1))
                                nc.vector.tensor_reduce(neg_max[:, o.n % 2, :], m_tile[:, o.n % 2, :, 0:o.Q + 1], AX.X,
                                                        ALU.max, negate=True).then_inc(s.negmax, 1)
                        if o.kind == "MT":
                            dve.wait_ge(s.ring_filled, base + o.ring + 1)
                            if o.n >= 2:
                                dve.wait_ge(mrows_in[o.n % 2], it * MROWS_N + 16 * NM * (o.n // 2))
                            src = ps[0:NM * HG * TPC, RING0 + o.ring % 3, 0:P // 2].bitcast(BF16)
                            nc.vector.tensor_copy(m_rows[:, o.n % 2, :], src).then_inc(s.ring_free, 1)
                        if o.kind == "YT":
                            dve.wait_ge(s.ring_filled, base + o.ring + 1)
                            y4 = ps[:, RING0 + o.ring % 3, :].rearrange("p (r h w) -> p r h w", r=TPC, h=HG)
                            if o.n >= 1:
                                dve.wait_ge(s.ring_free, base + YT_RING[o.n - 1] + 1)
                            nc.vector.reciprocal(recip[:], y4[:, :, :, DH]).then_inc(s.rcp, 1)
                            dve.wait_ge(s.rcp, it * NSTEP + o.n + 1)
                            dst = Y[:, TPC * o.Q:TPC * (o.Q + 1),
                                    bass.ds((it - PAIRS * L) * (2 * HG * DH) + o.buf * HG * DH, HG * DH)]
                            nc.vector.tensor_tensor(dst.rearrange("p r (h d) -> p r h d", h=HG), y4[:, :, :, 0:DH],
                                                    recip[:].rearrange("p r (h o) -> p r h o", o=1)
                                                    .broadcast_to([P, TPC, HG, DH]), ALU.mult).then_inc(s.ring_free, 1)

                    dve.wait_ge(s.mparts, it * (4 * NSTEP) + 4 * NSTEP)
                    dve.wait_ge(mrows_in[0], it * MROWS_N + MROWS_N)
                    dve.wait_ge(mrows_in[1], it * MROWS_N + MROWS_N)
                    dve.wait_ge(s.ring_free, base + RING_N)

                q = oproj[L]
                for u in range(NT // 2):
                    dve.wait_ge(q.o_ps, u + 1)
                    for t in range(2):
                        i = 2 * u + t
                        nc.vector.tensor_tensor(A[:, i, :], ps[:, 2 + u % 2, t * C:(t + 1) * C], row("b_o", L),
                                                ALU.add).then_inc(q.o_sb, 1)
                        dve.wait_ge(q.o_sb, i + 1)
                        stats_of(A[:, i, :], i, 0, q.st, turn[1 + 2 * L].stats_done)
                turn_vector(1 + 2 * L)

                f = ffn[L]

                def down_out(c):
                    dve.wait_ge(f.down, NI * (c + 1))
                    for t in range(TPC):
                        i = TPC * c + t
                        nc.vector.tensor_tensor(A[:, i, :], ps[:, 4 + t, 0:C], row("s_down", L),
                                                ALU.mult).then_inc(f.evac, 1)
                    for t in range(TPC):
                        i = TPC * c + t
                        dve.wait_ge(f.evac, i + 1)
                        stats_of(A[:, i, :], i, 0, f.st, turn[2 + 2 * L].stats_done)

                for u in range(NCH * NI):
                    c, i = divmod(u, NI)
                    dve.wait_ge(f.gate, u + 1)
                    if u >= 3:
                        dve.wait_ge(f.down, u - 2)
                    nc.vector.scalar_tensor_tensor(fuse_r[:, u % 3, :], ps[:, 2 + u % 2, :], col("s_up", layer=L, at=i),
                                                   gate_r[:, u % 2, :], ALU.mult, ALU.mult).then_inc(f.fuse, 1)
                    dve.wait_ge(f.fuse, u + 1)
                    nc.vector.tensor_tensor(frem_r[:, u % 3, :], fuse_r[:, u % 3, :], fuse_hi[:, u % 3, :],
                                            ALU.subtract).then_inc(f.rem, 1)
                    if i == 2 and c > 0:
                        down_out(c - 1)
                down_out(NCH - 1)
            turn_vector(4)

        @block.tensor
        def _(pe):
            def turn_tensor(k):
                tn = turn[k]
                for u in range(NT // 2):
                    if u >= 4:
                        if k % 2 == 0:
                            pe.wait_ge(tn.moved_a, u - 3)
                        else:
                            pe.wait_ge(tn.moved_v, u - 3)
                    for t in range(2):
                        i = 2 * u + t
                        pe.wait_ge(tn.xhat, i + 1)
                        for kc in range(KC):
                            ins = pe.transpose(ps[:, u % 4, kc * 2 * P + t * P:kc * 2 * P + (t + 1) * P],
                                               A[:, i, kc * P:(kc + 1) * P], ident[:])
                    ins.then_inc(tn.tpose, 1)

            def mm(o, a, b, first, last):
                return pe.matmul(o, a, b, start=first, stop=last)

            def unit_products(L, u):
                p = proj[L]
                kind, m, c = UNITS[L][u]
                b = 2 * (u % 2)
                cs = slice(c * CH, (c + 1) * CH)
                if u >= 2:
                    pe.wait_ge(p.val, u - 1)
                if kind == "kr":
                    for kc in range(KC):
                        ins = mm(ps[0:DR, b, :], w_kr[:, kc, :], XT[:, kc, cs], kc == 0, kc == KC - 1)
                elif kind == "q":
                    pe.wait_ge(p.zq_sb, c + 1)
                    pe.wait_ge(p.rot, 6)
                    ins = mm(ps[:, b, :], w_uq[:, m * P:(m + 1) * P], cq_t[0:DQ, cs], True, True)
                elif kind == "kn":
                    pe.wait_ge(p.zkv_sb, c + 1)
                    ins = mm(ps[:, b, :], w_kn, ckv_t[:, cs], True, True)
                else:
                    for kc in range(KC):
                        ins = mm(ps[:, b, :], w_qkv[:, kc, m * P:(m + 1) * P], XT[:, kc, cs], kc == 0, kc == KC - 1)
                ins.then_inc(p.u_ps, 1)

            pe.wait_ge(consts_in, 80)
            pe.wait_ge(setup_done, 3)
            pe.wait_ge(ones_done, 1)
            for L in range(2):
                p = proj[L]
                turn_tensor(2 * L)
                pe.wait_ge(turn[2 * L].moved_a, NT // 2)
                pe.wait_ge(w_in[L], 16 * (7 if L == 0 else 2))
                if L == 0:
                    for i in range(NT):
                        if i >= 2:
                            pe.wait_ge(p.down_sb, i - 1)
                        for kc in range(KC):
                            ins = mm(ps[:, 4 + i % 2, 0:DQ + DKV], XT[:, kc, i * P:(i + 1) * P], w_down[:, kc, :],
                                     kc == 0, kc == KC - 1)
                        ins.then_inc(p.down_ps, 1)
                    unit_products(0, 0)
                    unit_products(0, 1)
                    pe.wait_ge(p.down_sb, NT)
                    for g in range(NCH):
                        if g >= 2:
                            pe.wait_ge(p.zq_sb, g - 1)
                            pe.wait_ge(p.zkv_sb, g - 1)
                        b = 4 + 2 * (g % 2)
                        for t in range(TPC):
                            i = TPC * g + t
                            pe.wait_ge(p.z, 2 * i + 2)
                            pe.transpose(ps[0:DQ, b, t * P:(t + 1) * P], c_down[:, i, 0:DQ], ident[:])
                            ins = pe.transpose(ps[:, b + 1, t * P:(t + 1) * P], c_down[:, i, DQ:DQ + DKV], ident[:])
                        ins.then_inc(p.zt_ps, 1)
                    first = 2
                else:
                    first = 0
                for u in range(first, NU):
                    unit_products(L, u)
                if L == 0:
                    pe.wait_ge(p.zkv_sb, NCH)
                    pe.wait_ge(p.zq_sb, NCH)
                for u in range(VU):
                    if u >= 2:
                        pe.wait_ge(p.v_sb, u - 1)
                    for t in range(2):
                        ts = slice((2 * u + t) * P, (2 * u + t + 1) * P)
                        o = ps[:, 6 + u % 2, t * C:(t + 1) * C]
                        if L == 0:
                            ins = mm(o, ckv_t[:, ts], w_v0, True, True)
                        else:
                            for kc in range(KC):
                                ins = mm(o, XT[:, kc, ts], w_qkv[:, kc, 2 * C:3 * C], kc == 0, kc == KC - 1)
                    ins.then_inc(p.v_ps, 1)

                pe.wait_ge(p.val, NU)
                pe.wait_ge(p.v_sb, VU)
                pe.wait_ge(s.v_ones, L + 1)
                n_dma = 16 * (len(Q_PARTS) * NCH + len(K_PARTS) * (2 if L == 0 else 1))
                with pe.Fori(PAIRS * L, PAIRS * (L + 1)) as it:
                    pe.wait_ge(s.v_staged, it * 2 + 2)
                    seen = set()
                    for o in ORDER:
                        if o.ring is not None and o.ring >= 3:
                            pe.wait_ge(s.ring_free, it * RING_N + o.ring - 2)
                        if o.kind == "S":
                            if o.buf not in seen:
                                seen.add(o.buf)
                                pe.wait_ge(stack_in[L][o.buf], (it - PAIRS * L) * n_dma + n_dma)
                            n = CH if o.c < o.Q else P * (o.r + 1)
                            bank = ps[:, RING0 + o.ring % 3, :]
                            ins = mm(bank[:, 0:n], q_stack[0:NSTACK, o.buf, o.Q, o.h, o.r * P:(o.r + 1) * P],
                                     k_stack[0:NSTACK, o.buf, o.h, o.c * CH:o.c * CH + n], True, o.c < o.Q)
                            if o.c == o.Q:
                                ins = mm(bank[:, n - P:n], ident_bf[:], causal[:], False, True)
                            ins.then_inc(s.ring_filled, 1)
                        if o.kind == "MT":
                            pe.wait_ge(s.mparts, it * (4 * NSTEP) + 4 * (o.n + 1))
                            pe.transpose(ps[:, RING0 + o.ring % 3, 0:P // 2].bitcast(BF16),
                                         m_parts[:, o.n % 2, :], ident_bf[:]).then_inc(s.ring_filled, 1)
                        if o.kind == "T":
                            if o.k == 0 or o.n != n_now:
                                n_now = o.n
                                pe.wait_ge(mrows_in[o.n % 2], it * MROWS_N + 16 * NM * (o.n // 2 + 1))
                            if o.k >= 2:
                                pe.wait_ge(s.exp_done, it * T_N + o.k - 1)
                            for h in range(2):
                                hh = 2 * o.hp + h
                                ins = mm(psT[:, o.k % 2, h, o.off:CH], k_stack[0:KROWS, o.buf, hh, o.kt * P:(o.kt + 1) * P],
                                         q_stack[0:KROWS, o.buf, o.Q, hh, o.off:CH], True, True)
                            ins.then_inc(s.t_filled, 1)
                        if o.kind == "PV":
                            if o.sel is not None:
                                pe.wait_ge(s.selected, it * SEL_N + o.sel)
                            else:
                                pe.wait_ge(s.exp_done, it * T_N + 2 * o.j + 2)
                            if o.first and o.n > 0:
                                pe.wait_ge(s.y_evac, it * NSTEP + o.n)
                            for h in range(HG):
                                ins = mm(ps[32 * h:32 * h + VW, PV_BANK, o.off:CH], v_stage[:, o.buf, o.kt, h, :],
                                         probs[:, o.j % 3, h, o.off:CH], o.first, o.last)
                            ins.then_inc(s.pv_done, 1)
                        if o.kind == "YT":
                            pe.wait_ge(s.y_evac, it * NSTEP + o.n + 1)
                            for r in range(TPC):
                                ins = pe.transpose(ps[:, RING0 + o.ring % 3, r * P:(r + 1) * P],
                                                   y_chunk[:, o.n % 2, r * P:(r + 1) * P], ident[:])
                            ins.then_inc(s.ring_filled, 1)

                    pe.wait_ge(s.ring_free, it * RING_N + RING_N)
                    pe.wait_ge(s.exp_done, it * T_N + T_N)
                    pe.wait_ge(s.y_evac, it * NSTEP + NSTEP)

                q = oproj[L]

                def o_transpose(u):
                    if u >= 2:
                        pe.wait_ge(q.yt_sb, u - 1)
                    for t in range(2):
                        for kc in range(KC):
                            ins = pe.transpose(ps[:, u % 2, (2 * t + kc) * P:(2 * t + kc + 1) * P],
                                               Y[:, 2 * u + t, kc * P:(kc + 1) * P], ident[:])
                    ins.then_inc(q.yt_ps, 1)

                o_transpose(0)
                for u in range(NT // 2):
                    if u + 1 < NT // 2:
                        o_transpose(u + 1)
                    pe.wait_ge(q.yt_sb, u + 1)
                    if u >= 2:
                        pe.wait_ge(q.o_sb, 2 * (u - 1))
                    for t in range(2):
                        for kc in range(KC):
                            ins = mm(ps[:, 2 + u % 2, t * C:(t + 1) * C], y_t[:, u % 2, 2 * t + kc, :], w_o[:, kc, :],
                                     kc == 0, kc == KC - 1)
                    ins.then_inc(q.o_ps, 1)

                turn_tensor(1 + 2 * L)
                f = ffn[L]
                pe.wait_ge(turn[1 + 2 * L].moved_v, NT // 2)
                pe.wait_ge(wffn_done[L], 3)

                def down(u):
                    c, i = divmod(u, NI)
                    pe.wait_ge(f.lo, u + 1)
                    if i == 0 and c > 0:
                        pe.wait_ge(f.evac, TPC * c)
                    for t in range(TPC):
                        for k, part in enumerate((fuse_hi, frem_hi, flo_r)):
                            ins = mm(ps[:, 4 + t, 0:C], part[:, u % 3, t * P:(t + 1) * P], w_dn[:, i, :],
                                     i == 0 and k == 0, i == NI - 1 and k == 2)
                    ins.then_inc(f.down, 1)

                for u in range(NCH * NI):
                    c, i = divmod(u, NI)
                    if u >= 2:
                        pe.wait_ge(f.fuse, u - 1)
                    for w, bank in ((w_gate, u % 2), (w_up, 2 + u % 2)):
                        for kc in range(KC):
                            for k in range(2):
                                ins = mm(ps[:, bank, :], w[:, kc, i * P:(i + 1) * P],
                                         x16[:, k, kc, c * CH:(c + 1) * CH], kc == 0 and k == 0,
                                         kc == KC - 1 and k == 1)
                    ins.then_inc(f.gu_ps, 1)
                    if u >= 2:
                        down(u - 2)
                down(NCH * NI - 2)
                down(NCH * NI - 1)


def kernel(**inputs):
    import concourse.bacc as bacc
    from concourse.bass_utils import run_bass_kernel_spmd

    w = {k: np.asarray(v) for k, v in inputs.items()}
    swap = np.arange(C).reshape(H, DH).copy()
    swap[:, DN:] = np.roll(swap[:, DN:], DR // 2, axis=1)
    swap = swap.reshape(-1)

    inv_freq = (np.float32(1.0 / 10000.0) ** (np.arange(0, DR, 2, dtype=np.float32) / np.float32(DR))).astype(np.float32)
    freqs = np.arange(H, dtype=np.float32)[:, None] * inv_freq[None, :]
    cos, sin = np.cos(freqs).astype(np.float32), np.sin(freqs).astype(np.float32)
    cos_row = np.concatenate([np.ones((H, DN), np.float32), cos, cos], axis=1).reshape(-1)
    sin_row = np.concatenate([np.zeros((H, DN), np.float32), sin, -sin], axis=1).reshape(-1)

    def tiles(a):
        return np.ascontiguousarray(a.reshape(-1, P, a.shape[1]).transpose(1, 0, 2))

    u_kv = w["L0_attn_W_u_kv"].reshape(H, DN + DH, DKV)
    b_ukv = w["L0_attn_b_u_kv"].reshape(H, DN + DH)
    cols = np.zeros((P, NCOLS), np.float32)
    cols[:DQ, 0], cols[:DQ, 1] = w["L0_attn_q_norm_g"], w["L0_attn_q_norm_b"]
    cols[:, 2], cols[:, 3] = w["L0_attn_kv_norm_g"], w["L0_attn_kv_norm_b"]
    cols[:, 4:6] = w["L0_attn_b_u_q"].reshape(2, P).T
    cols[:, 6:8] = w["L0_attn_b_u_q"][swap].reshape(2, P).T
    cols[:, 8] = b_ukv[:, :DN].reshape(-1)
    cols[0:DR, 9] = w["L0_attn_b_d_kv"][DKV:]
    cols[:, 46:48], cols[:, 48:50] = cos_row.reshape(2, P).T, sin_row.reshape(2, P).T
    cols[:, 10:14] = w["L1_attn_b_qkv"][:2 * C].reshape(4, P).T
    for L in range(2):
        cols[:, COLS["s_gate"][L]:COLS["s_gate"][L] + NI] = w[f"L{L}_ffn_s_gate"].reshape(NI, P).T
        cols[:, COLS["s_up"][L]:COLS["s_up"][L] + NI] = w[f"L{L}_ffn_s_up"].reshape(NI, P).T
    rows = np.concatenate([w["L0_attn_b_d_q"], w["L0_attn_b_d_kv"][:DKV], b_ukv[:, DN:].reshape(-1), w["L0_attn_b_o"],
                           w["L1_attn_b_qkv"][2 * C:], w["L1_attn_b_out"], w["L0_ffn_s_down"],
                           w["L1_ffn_s_down"], cos_row, sin_row]).reshape(1, NROWS)
    bf = mybir.dt.np(BF16)
    arrays = {
        "x": w["L0_attn_x"].reshape(T, C),
        "cols": cols, "rows": rows,
        "ident": np.eye(P, dtype=np.float32), "ident_bf": np.eye(P).astype(bf),
        "causal": np.triu(np.full((P, P), MASKED), 1).astype(bf),
        "w_down": tiles(np.concatenate([w["L0_attn_W_d_q"], w["L0_attn_W_d_kv"][:DKV]]).T),
        "w_kr": tiles(w["L0_attn_W_d_kv"][DKV:].T),
        "w_uq": np.ascontiguousarray(w["L0_attn_W_u_q"].T),
        "w_uq_swap": np.ascontiguousarray(w["L0_attn_W_u_q"][swap].T),
        "w_kn": np.ascontiguousarray(u_kv[:, :DN].reshape(H * DN, DKV).T),
        "w_v0": np.ascontiguousarray(u_kv[:, DN:].reshape(H * DH, DKV).T),
        "w_qkv": tiles(w["L1_attn_w_qkv"].T),
        "w_o": np.stack([tiles(w["L0_attn_W_o"].T), tiles(w["L1_attn_w_out"].T)]),
    }
    for name, key in (("w_gate", "w_gate"), ("w_up", "w_up"), ("w_dn", "w_down")):
        arrays[name] = np.stack([tiles(w[f"L{L}_ffn_{key}"]).reshape(P, -1) for L in range(2)]).view(np.int32)

    nc = bacc.Bacc("TRN2", target_bir_lowering=False, num_devices=1)
    D = {k: nc.dram_tensor(f"in_{k}", v.shape, mybir.dt.from_np(v.dtype), kind="ExternalInput").ap()
         for k, v in arrays.items()}
    for name, n in (("q_parts", C), ("k_parts", C), ("kn_parts", H * DN), ("kr_parts", DR)):
        D[name] = nc.dram_tensor(name, (3, n, T), BF16, kind="Internal").ap()
    out = nc.dram_tensor("out_dram", (T, C), F32, kind="ExternalOutput").ap()
    build_program(nc, D, out)
    got = run_bass_kernel_spmd(nc, [{f"in_{k}": v for k, v in arrays.items()}], core_ids=[0])
    return got.results[0]["out_dram"].reshape(1, T, C)
```

```python
from contextlib import ExitStack
from collections import namedtuple

import numpy as np

import concourse.bass as bass
from concourse import mybir

ALU = mybir.AluOpType
ACT = mybir.ActivationFunctionType
AX = mybir.AxisListType
F32 = mybir.dt.float32
BF16 = mybir.dt.bfloat16
F16 = mybir.dt.float16
I8 = mybir.dt.int8

P = 128
T = 2048
C = 256
NT = T // P
KC = C // P
H = 16
DH = C // H
DQ = C // 3
DKV = C // 2
DN = DH // 2
DR = DH // 2
INTER = 1024
NI = INTER // P
EPS = 1e-5
CH = 512
NCH = T // CH
TPC = CH // P
HG = 4
NG = H // HG
Q_PARTS = (0, 0, 0, 1, 1, 2)
K_PARTS = (0, 1, 2, 0, 1, 0)
STACK_RUNS = ((0, 3), (3, 2), (5, 1))
HALF = 2
TH = T // HALF
CPH = NCH // HALF
NSTACK = DH * len(Q_PARTS)
NM = 3
KROWS = NSTACK + NM
VW = DH + 1
MASKED = -3.0e38
SCALE = 1.0 / DH ** 0.5

COLS = {"q_g": 0, "q_b": 1, "kv_g": 2, "kv_b": 3, "b_uq": 4, "b_uq_swap": 6, "b_kn": 8, "b_kr": 9,
        "b_qk1": 10, "s_gate": (14, 30), "s_up": (22, 38),
        "cos": 46, "sin": 48}
NCOLS = 50
ROWS = {"b_down": (0, DQ + DKV), "b_v": ((213, 256), (725, 256)), "b_o": ((469, 256), (981, 256)),
        "s_down": ((1237, 256), (1493, 256)), "cos": (1749, 256), "sin": (2005, 256)}
NROWS = 2261

PB = 4
RING = 3
SLOTS = 3
PE_LAT, SEM_NS, DVE_NS, LOAD_NS = 130, 60, 66, 20000
LEAD = 250

Step = namedtuple("Step", "kind n g Q h r c kt off first last hp ring k j sel", defaults=(None,) * 14)


def plan_attention():
    steps = [(g, Q) for g in range(NG) for Q in (range(NCH) if g % 2 == 0 else reversed(range(NCH)))]
    n_steps = len(steps)
    s_units = [(n, h, r, c) for n, (_, Q) in enumerate(steps) for h in range(HG) for r in range(TPC)
               for c in range(Q + 1)]
    kts = [list(range(TPC * Q, TPC * Q + TPC)) + list(range(TPC * Q)) for _, Q in steps]
    t_list = [(n, i, kt, hp) for n in range(n_steps) for i, kt in enumerate(kts[n]) for hp in range(2)]
    pv_list = [(n, i, kt) for n in range(n_steps) for i, kt in enumerate(kts[n])]
    size = [sum(HG * (TPC * Q + r + 1) for r in range(TPC)) for _, Q in steps]
    upto = [sum(size[:n]) for n in range(n_steps + 1)] + [sum(size)]
    s_done = t_done = 0
    order = []
    pe = dve = act = pool = 0.0
    ring_free = [0.0] * RING
    m_parts, m_rows, evac, exp_end, t_end = {}, {}, {}, {}, {}
    pair_free = [0.0] * 2
    v_free = 0.0
    ring = k = si = mt = yt = ti = pi = sel = sel_used = 0
    while yt < n_steps:
        cand = []
        if mt < n_steps and mt in m_parts:
            cand.append((0, max(m_parts[mt], ring_free[ring % RING]), "MT"))
        if yt in evac:
            cand.append((1, max(evac[yt], ring_free[ring % RING]), "YT"))
        if si < len(s_units) and s_units[si][0] < mt + 2:
            g = steps[s_units[si][0]][0]
            if g < 2 or g - 2 in t_end:
                n = t_list[ti][0] if ti < len(t_list) else n_steps - 1
                target = upto[n + 1] + (upto[n + 2] - upto[n + 1]) * (t_done - upto[n]) / size[n] + LEAD
                cand.append((2 if s_done < target else 5, max(ring_free[ring % RING], t_end[g - 2] + LOAD_NS if g >= 2 else 0), "S"))
        if pi < len(pv_list) and pi in exp_end:
            n, i, kt = pv_list[pi]
            if i > 0 or n == 0 or n - 1 in evac:
                cand.append((4.5, max(exp_end[pi], v_free if i == 0 else 0), "PV"))
        if ti < len(t_list):
            n, i, kt, hp = t_list[ti]
            if n in m_rows and ti // 2 < pi + SLOTS:
                cand.append((4, max(m_rows[n], pair_free[k % 2]), "T"))
        ready_now = [x for x in cand if x[1] <= pe + 1]
        _, ready, kind = min(ready_now) if ready_now else min(cand, key=lambda x: (x[1], x[0]))
        pe = max(pe, ready)
        if kind == "S":
            n, h, r, c = s_units[si]
            g, Q = steps[n]
            width = CH if c < Q else P * (r + 1)
            pe += width / 2.4 + (59 if c == Q else 6)
            dve = max(dve, pe + PE_LAT) + width / 0.96 + DVE_NS
            ring_free[ring % RING] = dve + SEM_NS
            si += 1
            s_done += width // P
            last = si == len(s_units) or s_units[si][0] != n
            order.append(Step("S", n, g, Q, h=h, r=r, c=c, last=last, ring=ring))
            ring += 1
            if last:
                dve += 150
                pool = max(pool, dve + 100) + 900
                m_parts[n] = pool + 100
        elif kind == "MT":
            g, Q = steps[mt]
            pe += 70
            dve = max(dve, pe + PE_LAT) + 150
            ring_free[ring % RING] = dve + SEM_NS
            order.append(Step("MT", mt, g, Q, ring=ring))
            ring += 1
            m_rows[mt] = dve + 2800
            mt += 1
        elif kind == "YT":
            g, Q = steps[yt]
            pe += 300
            dve = max(dve, pe + PE_LAT) + 500
            ring_free[ring % RING] = dve + SEM_NS
            order.append(Step("YT", yt, g, Q, ring=ring))
            ring += 1
            yt += 1
        elif kind == "T":
            n, i, kt, hp = t_list[ti]
            g, Q = steps[n]
            diag = kt >= TPC * Q
            off = P * (kt - TPC * Q) if diag else 0
            pe += 2 * (CH - off) / 2.4 + 12
            t_done += 2 * (CH - off) // P
            act = max(act, pe + PE_LAT) + 2 * (CH - off) / 1.2 + 55
            pair_free[k % 2] = act + SEM_NS
            last = i == len(kts[n]) - 1 and hp == 1
            order.append(Step("T", n, g, Q, kt=kt, off=off, hp=hp, k=k, j=ti // 2, first=diag, last=last))
            k += 1
            if hp == 1:
                exp_end[ti // 2] = act + SEM_NS
                if diag:
                    pool = max(pool, act + 60) + 600
                    exp_end[ti // 2] = pool + SEM_NS
                    sel += 1
            if last:
                t_end[g] = pe
            ti += 1
        else:
            n, i, kt = pv_list[pi]
            g, Q = steps[n]
            diag = kt >= TPC * Q
            off = P * (kt - TPC * Q) if diag else 0
            sel_used += diag
            pe += 4 * (CH - off) / 2.4 * 1.08
            last = i == len(kts[n]) - 1
            order.append(Step("PV", n, g, Q, kt=kt, off=off, first=i == 0, last=last, j=pi,
                              sel=sel_used if diag else None))
            if last:
                act = max(act, pe + PE_LAT) + 480
                v_free = evac[n] = act + SEM_NS
            pi += 1
    return steps, order


def build_program(nc, D, out):
    STEPS, ORDER = plan_attention()
    NSTEP = len(STEPS)
    RING_N = sum(1 for o in ORDER if o.ring is not None)
    T_N = sum(1 for o in ORDER if o.kind == "T")
    PV_N = sum(1 for o in ORDER if o.kind == "PV")
    SEL_N = max(o.sel for o in ORDER if o.kind == "PV" and o.sel is not None)
    MT_RING = {o.n: o.ring for o in ORDER if o.kind == "MT"}
    YT_RING = {o.n: o.ring for o in ORDER if o.kind == "YT"}
    LAST_T = {o.g: o.k for o in ORDER if o.kind == "T"}
    LAST_PV = {o.g: o.j for o in ORDER if o.kind == "PV"}

    with ExitStack() as ctx:
        def sb(name, shape, dt):
            return ctx.enter_context(nc.sbuf_tensor(name, shape, dt))

        def sem(name):
            return ctx.enter_context(nc.semaphore(name))

        X = sb("X", [P, NT, C], F32)
        region_a = sb("region_a", [P, NT * C], F32)
        region_v = sb("region_v", [P, NT * C], F32)
        region_vst = sb("region_vst", [P, 2 * NT * HG * VW], F32)
        region_p = sb("region_p", [P, SLOTS * HG * CH], F32)
        q_stack = sb("q_stack", [P, 2, HALF, HG, TH], BF16)
        k_stack = sb("k_stack", [P, 2, HALF, HG, TH], BF16)
        w_attn = sb("w_attn", [P, 2090], F32)
        w_ffn = sb("w_ffn", [P, 3 * KC * INTER], BF16)
        w_raw = sb("w_raw", [P, 3 * KC * INTER], I8)
        cols = sb("cols", [P, NCOLS], F32)
        rows = sb("rows", [P, NROWS], F32)
        ident = sb("ident", [P, P], F32)
        ident_bf = sb("ident_bf", [P, P], BF16)
        causal = sb("causal", [P, P], BF16)
        val = sb("val", [P, 2, CH], F32)
        rem = sb("rem", [P, 2, CH], F32)
        parts = sb("parts", [P, PB, 3, CH], BF16)
        y_chunk = sb("y_chunk", [P, 2, CH], F32)
        m_tile = sb("m_tile", [P, 2, HG * TPC, NCH], F32)
        neg_max = sb("neg_max", [P, 2, HG * TPC], F32)
        m_rem = sb("m_rem", [P, 2, HG * TPC], F32)
        m_parts = sb("m_parts", [P, 2, P], BF16)
        m_rows = sb("m_rows", [NM * HG * TPC, 2, P], BF16)
        recip = sb("recip", [P, TPC, HG], F32)
        stats = sb("stats", [P, NT, 2, 6], F32)
        mv = sb("mv", [P, NT, 2, 2], F32)
        std = sb("std", [P, NT, 2], F32)
        rstd = sb("rstd", [P, NT, 2], F32)
        eps = sb("eps", [P, 1], F32)
        ps = ctx.enter_context(nc.psum_tensor("ps", [P, 8, 512], F32))

        XT = region_a[:].rearrange("p (k t) -> p k t", k=KC)
        Y = region_a[:].rearrange("p (i c) -> p i c", i=NT)
        x16 = region_a[:].bitcast(F16).rearrange("p (s k t) -> p s k t", s=2, k=KC)
        V = region_v[:].rearrange("p (i c) -> p i c", i=NT)
        v_stage = region_vst[:].rearrange("p (b i h w) -> p b i h w", b=2, i=NT, h=HG)
        probs = region_p[:].rearrange("p (s h q) -> p s h q", s=SLOTS, h=HG)
        A = region_p[:, 0:NT * C].rearrange("p (i c) -> p i c", i=NT)
        c_down = region_p[:, 0:NT * (DQ + DKV)].rearrange("p (i c) -> p i c", i=NT)
        q_flat = q_stack[:].rearrange("p b s h t -> p (b s h t)").bitcast(F32)
        cq_t, ckv_t = (q_flat[:, i * T:(i + 1) * T] for i in (2, 3))
        y_t = q_flat[:, 0:2 * CH].rearrange("p (b k t) -> p b k t", b=2, k=KC * 2)
        gate_r = region_v[:, 0:2 * CH].rearrange("p (s t) -> p s t", s=2)
        fuse_r = region_v[:, 2 * CH:5 * CH].rearrange("p (s t) -> p s t", s=3)
        frem_r = region_v[:, 5 * CH:8 * CH].rearrange("p (s t) -> p s t", s=3)
        flo_r = region_vst[:, 0:3 * CH // 2].bitcast(BF16).rearrange("p (s t) -> p s t", s=3)
        fuse_hi = fuse_r.bitcast(BF16).rearrange("p s (t two) -> p s t two", two=2)[:, :, :, 1]
        frem_hi = frem_r.bitcast(BF16).rearrange("p s (t two) -> p s t two", two=2)[:, :, :, 1]
        w_down = w_attn[:, 0:KC * 213].rearrange("p (k c) -> p k c", k=KC)
        w_kr = w_attn[:, 426:682].rearrange("p (k c) -> p k c", k=KC)
        w_uq = w_attn[0:DQ, 682:938]
        w_uq_swap = w_attn[0:DQ, 938:1194]
        w_kn = w_attn[:, 1194:1322]
        w_v0 = w_attn[:, 1322:1578]
        w_qkv = w_attn[:, 0:KC * 3 * C].rearrange("p (k c) -> p k c", k=KC)
        w_o = w_attn[:, 1578:2090].rearrange("p (k c) -> p k c", k=KC)
        w_gate, w_up = (w_ffn[:, i * KC * INTER:(i + 1) * KC * INTER].rearrange("p (k c) -> p k c", k=KC)
                        for i in range(2))
        w_dn = w_ffn[:, 2 * KC * INTER:].rearrange("p (k c) -> p k c", k=NI)
        psT = ps[:, 0:4, :].rearrange("p (b h) q -> p b h q", b=2)
        RING0, PV_BANK = 4, 7

        def col(name, width=1, n=P, layer=None, at=0):
            c = COLS[name] if layer is None else COLS[name][layer]
            return cols[0:n, c + at:c + at + width]

        def row(name, layer=None):
            a, n = ROWS[name] if layer is None else ROWS[name][layer]
            return rows[:, a:a + n]

        ident_in = sem("ident_in")
        consts_in = sem("consts_in")
        rows_in = sem("rows_in")
        x_in = [sem(f"x_in{i}") for i in range(4)]
        w_in = [sem(f"w_in{L}") for L in range(2)]
        wraw_in = [sem(f"wraw_in{L}") for L in range(2)]
        wffn_done = [sem(f"wffn_done{L}") for L in range(2)]
        setup_done = sem("setup_done")
        ones_done = sem("ones_done")
        out_stored = sem("out_stored")

        def Sems(stage, *names):
            return namedtuple(stage, names)(*[sem(f"{stage}_{n}") for n in names])

        TURN_IN = ("stats_done", "std_done", "rstd_done", "normed", "added")
        TURN_OUT = ("stats2", "var2", "std2", "rstd2", "xhat", "tpose", "moved_a", "moved_v")
        turn = [Sems(f"turn{k}", *(TURN_IN if k > 0 else ()), *(TURN_OUT if k < 4 else ())) for k in range(5)]
        SPLIT = ("u_ps", "val", "hi", "rem", "mid", "lo", "v_ps", "v_sb")
        proj = [Sems("proj0", *SPLIT, "rot", "down_ps", "down_sb", "stat", "var", "std", "rstd", "z", "zt_ps", "zq_sb",
                     "zkv_sb"), Sems("proj1", *SPLIT)]
        parts_stored = [[sem(f"parts_stored{L}{b}") for b in range(PB)] for L in range(2)]
        stack_in = [[sem(f"stack{L}{b}") for b in range(2)] for L in range(2)]
        stack_half = [sem(f"stack_half{L}") for L in range(2)]
        s = Sems("att", "ring_filled", "ring_free", "negmax", "mparts", "t_filled", "exp_done", "selected",
                 "pv_done", "y_evac", "rcp", "v_staged", "v_ones")
        mrows_in = [sem(f"mrows_in{i}") for i in range(2)]
        MROWS_N = 16 * HG * (NSTEP // 2)
        oproj = [Sems(f"oproj{L}", "yt_ps", "yt_sb", "o_ps", "o_sb", "st") for L in range(2)]
        ffn = [Sems(f"ffn{L}", "gu_ps", "gate", "fuse", "rem", "lo", "down", "evac", "st") for L in range(2)]

        UNITS = [
            [(kind, 0, c) for c in range(NCH) for kind in ("kr", "q", "kn")] + [("q", 1, c) for c in range(NCH)],
            [("qk", m, c) for c in range(NCH) for m in (0, 2)] + [("qk", m, c) for c in range(NCH) for m in (1, 3)],
        ]
        NU = 16
        VU = NT // 2
        EARLY = (12, 8)

        def v_after(L, u):
            if u < EARLY[L]:
                return range(0)
            n = VU // (NU - EARLY[L])
            return range((u - EARLY[L]) * n, (u - EARLY[L] + 1) * n)
        def unit_dram(L, u):
            kind, m, c = UNITS[L][u]
            if kind == "qk":
                kind, m = ("q", m) if m < 2 else ("k", m - 2)
            half, ts = c // CPH, slice(c % CPH * CH, (c % CPH + 1) * CH)
            if kind in ("kn", "kr"):
                d = slice(0, DN) if kind == "kn" else slice(DN, DH)
                return D["k_parts0"][half, :, d, :, ts].rearrange("s d h t -> (d h) s t")
            return D["q_parts" if kind == "q" else "k_parts1"][m, half, :, :, :, ts].rearrange("s d h t -> (d h) s t")

        KPH = NT // HALF

        def q_at(o):
            return o.Q % CPH * CH

        block = ctx.enter_context(nc.Block())

        @block.sync
        def _(sp):
            xin = D["x"].rearrange("(i p) c -> p i c", p=P)
            for g in range(4):
                sp.dma_start(X[:, 4 * g:4 * g + 4, :], xin[:, 4 * g:4 * g + 4, :]).then_inc(x_in[g], 16)

            for L in range(2):
                def stack_dmas(g, halves=range(HALF)):
                    dmas = []
                    h0 = g % 2 * HG
                    for half in halves:
                        for first, n in STACK_RUNS:
                            rows_ = slice(first * DH, (first + n) * DH)
                            part = Q_PARTS[first]
                            src = D["q_parts"][g // 2, half, part:part + 1, :, h0:h0 + HG, :]
                            dmas.append((q_stack[rows_, g % 2, half, :, :].rearrange("p h t -> p (h t)"),
                                         src.rearrange("s d h t -> s d (h t)").broadcast_to([n, DH, HG * TH])))
                            src = (D["k_parts0"][half, 0:n, :, g * HG:(g + 1) * HG, :] if L == 0 else
                                   D["k_parts1"][g // 2, half, 0:n, :, h0:h0 + HG, :])
                            dmas.append((k_stack[rows_, g % 2, half, :, :].rearrange("p h t -> p (h t)"),
                                         src.rearrange("s d h t -> s d (h t)")))
                    return dmas

                def load(b, dma, done=None):
                    sp.dma_start(dma[0], dma[1]).then_inc(done or stack_in[L][b], 16)

                def parts_complete(n):
                    for b in range(PB):
                        sp.wait_ge(parts_stored[L][b], 16 * ((n - b + PB - 1) // PB))

                for u in range(NU):
                    sp.wait_ge(proj[L].lo, u + 1)
                    sp.dma_start(unit_dram(L, u), parts[:, u % PB, :, :]).then_inc(parts_stored[L][u % PB], 16)
                    for half in range(HALF):
                        n = EARLY[L] * (half + 1) // HALF
                        if u == n + 1:
                            parts_complete(n)
                            for dma in stack_dmas(0, (half,)):
                                load(0, dma, stack_half[L] if half == 0 else None)
                parts_complete(NU)
                if L == 0:
                    sp.wait_ge(proj[L].v_ps, VU)
                queue = [(1, dma) for dma in stack_dmas(1)]
                for o in ORDER:
                    if o.kind == "MT":
                        sp.wait_ge(s.ring_free, L * RING_N + o.ring + 1)
                        for h in range(HG):
                            dst = q_stack[NSTACK:KROWS, o.g % 2, o.Q // CPH, h, q_at(o):q_at(o) + CH].rearrange(
                                "m (r t) -> m r t", r=TPC)
                            src = m_rows[h * NM * TPC:(h + 1) * NM * TPC, o.n % 2, :]
                            sp.dma_start(dst, src).then_inc(mrows_in[o.n % 2], 16)
                    if o.kind == "T" and o.k == LAST_T[o.g] and o.g + 2 < NG:
                        sp.wait_ge(s.t_filled, L * T_N + o.k + 1)
                        queue = [(o.g % 2, dma) for dma in stack_dmas(o.g + 2)]
                    elif queue and o.kind == "T":
                        load(*queue.pop(0))

            for g in range(4):
                sp.wait_ge(turn[4].added, 4 * g + 4)
                sp.dma_start(out.rearrange("(i p) c -> p i c", p=P)[:, 4 * g:4 * g + 4, :],
                             X[:, 4 * g:4 * g + 4, :]).then_inc(out_stored, 16)
            sp.wait_ge(out_stored, 64)

        @block.gpsimd
        def _(pool):
            def load_weights(L):
                if L == 0:
                    pool.dma_start(w_down, D["w_down"]).then_inc(w_in[0], 16)
                    pool.dma_start(w_kr, D["w_kr"]).then_inc(w_in[0], 16)
                    pool.dma_start(w_uq, D["w_uq"]).then_inc(w_in[0], 16)
                    pool.dma_start(w_uq_swap, D["w_uq_swap"]).then_inc(w_in[0], 16)
                    pool.dma_start(w_kn, D["w_kn"]).then_inc(w_in[0], 16)
                    pool.dma_start(w_v0, D["w_v0"]).then_inc(w_in[0], 16)
                else:
                    pool.wait_ge(oproj[0].o_ps, NT // 2)
                    pool.dma_start(w_qkv, D["w_qkv"]).then_inc(w_in[1], 16)
                pool.dma_start(w_o, D["w_o"][L]).then_inc(w_in[L], 16)

            def load_ffn(L):
                if L == 1:
                    pool.wait_ge(wffn_done[0], 3)
                raw = w_raw[:].bitcast(mybir.dt.int32).rearrange("p (s c) -> p s c", s=3)
                for s, name in enumerate(("w_gate", "w_up", "w_dn")):
                    pool.dma_start(raw[:, s, :], D[name][L]).then_inc(wraw_in[L], 16)

            pool.dma_start(rows[:], D["rows"].broadcast_to([P, NROWS])).then_inc(rows_in, 16)
            load_weights(0)
            load_ffn(0)
            nc.gpsimd.memset(k_stack[NSTACK:KROWS, :, :, :, :], 1.0).then_inc(ones_done, 1)
            pool.wait_ge(ones_done, 1)

            def split_lo(L, u):
                pool.wait_ge(proj[L].mid, u + 1)
                nc.gpsimd.tensor_tensor(parts[:, u % PB, 2, :], rem[:, u % 2, :], parts[:, u % PB, 1, :],
                                        ALU.subtract).then_inc(proj[L].lo, 1)

            def add_residual(k, i):
                pool.wait_ge(turn[k].normed, i + 1)
                nc.gpsimd.tensor_tensor(X[:, i, :], X[:, i, :], A[:, i, :], ALU.add).then_inc(turn[k].added, 1)

            def stage_ones(L):
                nc.gpsimd.memset(v_stage[:, :, :, :, DH:VW], 1.0).then_inc(s.v_ones, 1)

            for L in range(2):
                if L == 0:
                    stage_ones(0)
                for u in range(NU):
                    split_lo(L, u)
                pool.wait_ge(proj[L].v_sb, VU)
                if L == 1:
                    stage_ones(1)

                def stage_values(g):
                    nc.gpsimd.tensor_copy(v_stage[:, g % 2, :, :, 0:DH],
                                          V[:, :, g * HG * DH:(g + 1) * HG * DH].rearrange("p i (h d) -> p i h d", h=HG)
                                          ).then_inc(s.v_staged, 1)

                stage_values(0)
                stage_values(1)
                for o in ORDER:
                    if o.kind == "S" and o.last:
                        nm, mr = (m[:, o.n % 2, :].rearrange("p (h r) -> p h r", h=HG) for m in (neg_max, m_rem))
                        mp = m_parts[:, o.n % 2, 0:NM * HG * TPC].rearrange("p (h s r) -> p s h r", s=NM, h=HG)
                        c0 = 4 * (L * NSTEP + o.n)
                        pool.wait_ge(s.negmax, L * NSTEP + o.n + 1)
                        if o.n >= 2:
                            pool.wait_ge(s.ring_filled, L * RING_N + MT_RING[o.n - 2] + 1)
                        nc.gpsimd.tensor_copy(mp[:, 0, :, :], nm).then_inc(s.mparts, 1)
                        pool.wait_ge(s.mparts, c0 + 1)
                        nc.gpsimd.tensor_tensor(mr, nm, mp[:, 0, :, :], ALU.subtract).then_inc(s.mparts, 1)
                        pool.wait_ge(s.mparts, c0 + 2)
                        nc.gpsimd.tensor_copy(mp[:, 1, :, :], mr).then_inc(s.mparts, 1)
                        pool.wait_ge(s.mparts, c0 + 3)
                        nc.gpsimd.tensor_tensor(mp[:, 2, :, :], mr, mp[:, 1, :, :], ALU.subtract).then_inc(s.mparts, 1)
                    if o.kind == "T" and o.first and o.hp == 1:
                        pool.wait_ge(s.exp_done, L * T_N + o.k + 1)
                        blk = probs[:, o.j % SLOTS, :, o.off:o.off + P]
                        nc.gpsimd.affine_select(out=blk, in_=blk, compare_op=ALU.is_ge, fill=0.0, base=0,
                                                pattern=[[0, HG], [1, P]], channel_multiplier=-1
                                                ).then_inc(s.selected, 1)
                    if o.kind == "PV" and o.j == LAST_PV[o.g] and o.g + 2 < NG:
                        pool.wait_ge(s.pv_done, L * PV_N + o.j + 1)
                        stage_values(o.g + 2)
                if L == 0:
                    load_weights(1)
                for i in range(NT):
                    add_residual(1 + 2 * L, i)
                for u in range(NCH * NI):
                    pool.wait_ge(ffn[L].rem, u + 1)
                    if u >= 3:
                        pool.wait_ge(ffn[L].down, u - 2)
                    nc.gpsimd.tensor_tensor(flo_r[:, u % 3, :], frem_r[:, u % 3, :], frem_hi[:, u % 3, :],
                                            ALU.subtract).then_inc(ffn[L].lo, 1)
                if L == 0:
                    load_ffn(1)
                for i in range(NT):
                    add_residual(2 + 2 * L, i)

        @block.scalar
        def _(act):
            def turn_scalar(k):
                tn = turn[k]
                if k > 0:
                    act.wait_ge(tn.stats_done, NT)
                    nc.scalar.activation(std[:, :, 0], mv[:, :, 0, 1], ACT.Sqrt, bias=eps[:]).then_inc(tn.std_done, 1)
                if k == 4:
                    return
                act.wait_ge(tn.stats2, NT)
                nc.scalar.activation(std[:, :, 1], mv[:, :, 1, 1], ACT.Sqrt, bias=eps[:]).then_inc(tn.std2, 1)
                for u in range(NT // 2):
                    act.wait_ge(tn.tpose, u + 1)
                    src = ps[:, u % 4, :].rearrange("p (k t) -> p k t", k=KC)
                    if k % 2 == 0:
                        nc.scalar.copy(XT[:, :, u * 2 * P:(u + 1) * 2 * P], src).then_inc(tn.moved_a, 1)
                    else:
                        nc.scalar.copy(x16[:, 0, :, u * 2 * P:(u + 1) * 2 * P], src).then_inc(tn.moved_a, 1)

            def convert_ffn(L):
                act.wait_ge(wraw_in[L], 48)
                if L == 1:
                    act.wait_ge(ffn[0].down, NCH * NI)
                n = KC * INTER
                for k in range(3):
                    nc.scalar.copy(w_ffn[:, k * n:(k + 1) * n], w_raw[:, k * n:(k + 1) * n]).then_inc(wffn_done[L], 1)

            def split_hi(L, u):
                act.wait_ge(proj[L].val, u + 1)
                if u >= PB:
                    act.wait_ge(parts_stored[L][u % PB], 16 * (u // PB))
                nc.scalar.copy(parts[:, u % PB, 0, :], val[:, u % 2, :]).then_inc(proj[L].hi, 1)

            def split_mid(L, u):
                act.wait_ge(proj[L].rem, u + 1)
                nc.scalar.copy(parts[:, u % PB, 1, :], rem[:, u % 2, :]).then_inc(proj[L].mid, 1)

            act.dma_start(ident[:], D["ident"]).then_inc(ident_in, 16)
            act.dma_start(cols[:], D["cols"]).then_inc(consts_in, 16)
            act.dma_start(ident_bf[:], D["ident_bf"]).then_inc(consts_in, 16)
            act.dma_start(causal[:], D["causal"]).then_inc(consts_in, 16)
            act.wait_ge(setup_done, 3)
            act.wait_ge(consts_in, 48)
            for L in range(2):
                turn_scalar(2 * L)
                convert_ffn(L)
                if L == 0:
                    p = proj[0]
                    act.wait_ge(p.stat, 2 * NT)
                    nc.scalar.activation(std[:], mv[:, :, :, 1], ACT.Sqrt, bias=eps[:]).then_inc(p.std, 1)
                    for g in range(NCH):
                        act.wait_ge(p.zt_ps, g + 1)
                        nc.scalar.activation(cq_t[0:DQ, g * CH:(g + 1) * CH], ps[0:DQ, 4 + 2 * (g % 2), :], ACT.Identity,
                                             scale=col("q_g", n=DQ), bias=col("q_b", n=DQ)).then_inc(p.zq_sb, 1)
                for u in range(NU):
                    split_hi(L, u)
                    if u > 0:
                        split_mid(L, u - 1)
                split_mid(L, NU - 1)

                for o in ORDER:
                    if o.kind == "T":
                        act.wait_ge(s.t_filled, L * T_N + o.k + 1)
                        if o.j >= SLOTS:
                            act.wait_ge(s.pv_done, L * PV_N + o.j - SLOTS + 1)
                        nc.scalar.activation(probs[:, o.j % SLOTS, 2 * o.hp:2 * o.hp + 2, o.off:CH],
                                             psT[:, o.k % 2, :, o.off:CH], ACT.Exp, scale=SCALE).then_inc(s.exp_done, 1)
                    if o.kind == "PV" and o.last:
                        act.wait_ge(s.pv_done, L * PV_N + o.j + 1)
                        if o.n >= 2:
                            act.wait_ge(s.ring_filled, L * RING_N + YT_RING[o.n - 2] + 1)
                        nc.scalar.copy(y_chunk[:, o.n % 2, :], ps[:, PV_BANK, :]).then_inc(s.y_evac, 1)

                for u in range(NT // 2):
                    act.wait_ge(oproj[L].yt_ps, u + 1)
                    if u >= 2:
                        act.wait_ge(oproj[L].o_ps, u - 1)
                    nc.scalar.copy(y_t[:, u % 2, :, :], ps[:, u % 2, :].rearrange("p (k t) -> p k t", t=P)
                                   ).then_inc(oproj[L].yt_sb, 1)
                turn_scalar(1 + 2 * L)
                f = ffn[L]
                for u in range(NCH * NI):
                    act.wait_ge(f.gu_ps, u + 1)
                    if u >= 2:
                        act.wait_ge(f.fuse, u - 1)
                    it_ = u % NI
                    nc.scalar.activation(gate_r[:, u % 2, :], ps[:, u % 2, :], ACT.Silu,
                                         scale=col("s_gate", layer=L, at=it_)).then_inc(f.gate, 1)
            turn_scalar(4)

        @block.vector
        def _(dve):
            def stats_of(src, i, which, after, done):
                nc.vector.bn_stats(stats[:, i, which, :], src).then_inc(after, 1)
                dve.wait_ge(after, i + 1)
                nc.vector.bn_aggr(mv[:, i, which, :], stats[:, i, which, :]).then_inc(done, 1)

            def turn_vector(k):
                tn = turn[k]
                if k > 0:
                    dve.wait_ge(tn.std_done, 1)
                    nc.vector.reciprocal(rstd[:, :, 0], std[:, :, 0]).then_inc(tn.rstd_done, 1)
                    dve.wait_ge(tn.rstd_done, 1)
                    for i in range(NT):
                        nc.vector.tensor_scalar(A[:, i, :], A[:, i, :], mv[:, i, 0, 0:1], rstd[:, i, 0:1], ALU.subtract,
                                                ALU.mult).then_inc(tn.normed, 1)
                if k == 4:
                    return
                for i in range(NT):
                    if k > 0:
                        dve.wait_ge(tn.added, i + 1)
                    else:
                        dve.wait_ge(x_in[i // 4], 16)
                    stats_of(X[:, i, :], i, 1, tn.var2, tn.stats2)
                dve.wait_ge(tn.std2, 1)
                nc.vector.reciprocal(rstd[:, :, 1], std[:, :, 1]).then_inc(tn.rstd2, 1)
                dve.wait_ge(tn.rstd2, 1)
                for i in range(NT):
                    nc.vector.tensor_scalar(A[:, i, :], X[:, i, :], mv[:, i, 1, 0:1], rstd[:, i, 1:2], ALU.subtract,
                                            ALU.mult).then_inc(tn.xhat, 1)
                if k % 2 == 1:
                    for u in range(NT // 2):
                        dve.wait_ge(tn.moved_a, u + 1)
                        sl = slice(u * 2 * P, (u + 1) * 2 * P)
                        nc.vector.tensor_tensor(x16[:, 1, :, sl], ps[:, u % 4, :].rearrange("p (k t) -> p k t", k=KC),
                                                x16[:, 0, :, sl], ALU.subtract).then_inc(tn.moved_v, 1)

            def unit_value(L, u):
                p = proj[L]
                kind, m, c = UNITS[L][u]
                dve.wait_ge(p.u_ps, u + 1)
                if u >= 2:
                    dve.wait_ge(p.rem, u - 1)
                dst = val[:, u % 2, :]
                b = u % 4
                bias = {"kr": col("b_kr"), "q": col("b_uq", at=m), "kn": col("b_kn"),
                        "qk": col("b_qk1", at=m)}[kind]
                nc.vector.tensor_scalar(dst, ps[:, b, :], bias, None, ALU.add).then_inc(p.val, 1)

            def unit_rem(L, u):
                p = proj[L]
                dve.wait_ge(p.hi, u + 1)
                if u >= 2:
                    dve.wait_ge(p.lo, u - 1)
                nc.vector.tensor_tensor(rem[:, u % 2, :], val[:, u % 2, :], parts[:, u % PB, 0, :],
                                        ALU.subtract).then_inc(p.rem, 1)

            def v_value(L, v):
                dve.wait_ge(proj[L].v_ps, v + 1)
                for t in range(2):
                    ins = nc.vector.tensor_tensor(V[:, 2 * v + t, :], ps[:, 6 + v % 2, t * C:(t + 1) * C],
                                                  row("b_v", L), ALU.add)
                ins.then_inc(proj[L].v_sb, 1)

            nc.vector.memset(m_parts[:], 0.0).then_inc(setup_done, 1)
            nc.vector.memset(eps[:], EPS).then_inc(setup_done, 1)
            nc.vector.memset(ps[:, PV_BANK, :], 0.0).then_inc(setup_done, 1)
            for L in range(2):
                p = proj[L]
                turn_vector(2 * L)
                if L == 0:
                    dve.wait_ge(consts_in, 48)
                    dve.wait_ge(rows_in, 16)
                    dve.wait_ge(w_in[0], 16 * 7)
                    for a, name in ((w_uq, "cos"), (w_uq_swap, "sin")):
                        nc.vector.tensor_tensor(a, a, row(name)[0:DQ, :], ALU.mult).then_inc(p.rot, 1)
                    for a, name in (("b_uq", "cos"), ("b_uq_swap", "sin")):
                        nc.vector.tensor_tensor(col(a, 2), col(a, 2), col(name, 2), ALU.mult).then_inc(p.rot, 1)
                    dve.wait_ge(p.rot, 4)
                    nc.vector.tensor_tensor(w_uq, w_uq, w_uq_swap, ALU.add).then_inc(p.rot, 1)
                    nc.vector.tensor_tensor(col("b_uq", 2), col("b_uq", 2), col("b_uq_swap", 2), ALU.add
                                            ).then_inc(p.rot, 1)
                    dve.wait_ge(p.rot, 6)
                    for i in range(NT):
                        dve.wait_ge(p.down_ps, i + 1)
                        if i == 0:
                            dve.wait_ge(turn[0].tpose, NT // 2)
                        nc.vector.tensor_tensor(c_down[:, i, :], ps[:, 4 + i % 2, 0:DQ + DKV], row("b_down"),
                                                ALU.add).then_inc(p.down_sb, 1)
                        dve.wait_ge(p.down_sb, i + 1)
                        for w, cs in enumerate((slice(0, DQ), slice(DQ, DQ + DKV))):
                            nc.vector.bn_stats(stats[:, i, w, :], c_down[:, i, cs]).then_inc(p.var, 1)
                        dve.wait_ge(p.var, 2 * i + 2)
                        for w in range(2):
                            nc.vector.bn_aggr(mv[:, i, w, :], stats[:, i, w, :]).then_inc(p.stat, 1)
                    dve.wait_ge(p.std, 1)
                    nc.vector.reciprocal(rstd[:], std[:]).then_inc(p.rstd, 1)
                    dve.wait_ge(p.rstd, 1)
                    for i in range(NT):
                        for w, cs in enumerate((slice(0, DQ), slice(DQ, DQ + DKV))):
                            nc.vector.tensor_scalar(c_down[:, i, cs], c_down[:, i, cs], mv[:, i, w, 0:1],
                                                    rstd[:, i, w:w + 1], ALU.subtract, ALU.mult).then_inc(p.z, 1)
                    for g in range(NCH):
                        dve.wait_ge(p.zt_ps, g + 1)
                        nc.vector.tensor_scalar(ckv_t[:, g * CH:(g + 1) * CH], ps[:, 5 + 2 * (g % 2), :], col("kv_g"),
                                                col("kv_b"), ALU.mult, ALU.add).then_inc(p.zkv_sb, 1)
                for u in range(NU):
                    unit_value(L, u)
                    if u > 0:
                        unit_rem(L, u - 1)
                    for v in v_after(L, u):
                        v_value(L, v)
                unit_rem(L, NU - 1)

                base = L * RING_N
                for o in ORDER:
                    if o.kind == "S":
                        n = CH if o.c < o.Q else P * (o.r + 1)
                        if o.h == o.r == o.c == 0 and o.n >= 2:
                            dve.wait_ge(s.negmax, L * NSTEP + o.n - 1)
                        dve.wait_ge(s.ring_filled, base + o.ring + 1)
                        nc.vector.tensor_reduce(m_tile[:, o.n % 2, o.h * TPC + o.r, o.c:o.c + 1],
                                                ps[:, RING0 + o.ring % RING, 0:n], AX.X, ALU.max).then_inc(s.ring_free, 1)
                        if o.last:
                            dve.wait_ge(s.ring_free, base + o.ring + 1)
                            if o.n >= 2:
                                dve.wait_ge(s.mparts, 4 * (L * NSTEP + o.n - 1))
                            nc.vector.tensor_reduce(neg_max[:, o.n % 2, :], m_tile[:, o.n % 2, :, 0:o.Q + 1], AX.X,
                                                    ALU.max, negate=True).then_inc(s.negmax, 1)
                    if o.kind == "MT":
                        dve.wait_ge(s.ring_filled, base + o.ring + 1)
                        if o.n >= 2:
                            dve.wait_ge(mrows_in[o.n % 2], L * MROWS_N + 16 * HG * (o.n // 2))
                        src = ps[0:NM * HG * TPC, RING0 + o.ring % RING, 0:P // 2].bitcast(BF16)
                        nc.vector.tensor_copy(m_rows[:, o.n % 2, :], src).then_inc(s.ring_free, 1)
                    if o.kind == "YT":
                        dve.wait_ge(s.ring_filled, base + o.ring + 1)
                        y4 = ps[:, RING0 + o.ring % RING, :].rearrange("p (r h w) -> p r h w", r=TPC, h=HG)
                        if o.n >= 1:
                            dve.wait_ge(s.ring_free, base + YT_RING[o.n - 1] + 1)
                        nc.vector.reciprocal(recip[:], y4[:, :, :, DH]).then_inc(s.rcp, 1)
                        dve.wait_ge(s.rcp, L * NSTEP + o.n + 1)
                        dst = Y[:, TPC * o.Q:TPC * (o.Q + 1), o.g * HG * DH:(o.g + 1) * HG * DH]
                        nc.vector.tensor_tensor(dst.rearrange("p r (h d) -> p r h d", h=HG), y4[:, :, :, 0:DH],
                                                recip[:].rearrange("p r (h o) -> p r h o", o=1)
                                                .broadcast_to([P, TPC, HG, DH]), ALU.mult).then_inc(s.ring_free, 1)

                q = oproj[L]
                for u in range(NT // 2):
                    dve.wait_ge(q.o_ps, u + 1)
                    for t in range(2):
                        i = 2 * u + t
                        nc.vector.tensor_tensor(A[:, i, :], ps[:, 2 + u % 2, t * C:(t + 1) * C], row("b_o", L),
                                                ALU.add).then_inc(q.o_sb, 1)
                        dve.wait_ge(q.o_sb, i + 1)
                        stats_of(A[:, i, :], i, 0, q.st, turn[1 + 2 * L].stats_done)
                turn_vector(1 + 2 * L)

                f = ffn[L]

                def down_out(c):
                    dve.wait_ge(f.down, NI * (c + 1))
                    for t in range(TPC):
                        i = TPC * c + t
                        nc.vector.tensor_tensor(A[:, i, :], ps[:, 4 + t, 0:C], row("s_down", L),
                                                ALU.mult).then_inc(f.evac, 1)
                    for t in range(TPC):
                        i = TPC * c + t
                        dve.wait_ge(f.evac, i + 1)
                        stats_of(A[:, i, :], i, 0, f.st, turn[2 + 2 * L].stats_done)

                for u in range(NCH * NI):
                    c, i = divmod(u, NI)
                    dve.wait_ge(f.gate, u + 1)
                    if u >= 3:
                        dve.wait_ge(f.down, u - 2)
                    nc.vector.scalar_tensor_tensor(fuse_r[:, u % 3, :], ps[:, 2 + u % 2, :], col("s_up", layer=L, at=i),
                                                   gate_r[:, u % 2, :], ALU.mult, ALU.mult).then_inc(f.fuse, 1)
                    dve.wait_ge(f.fuse, u + 1)
                    nc.vector.tensor_tensor(frem_r[:, u % 3, :], fuse_r[:, u % 3, :], fuse_hi[:, u % 3, :],
                                            ALU.subtract).then_inc(f.rem, 1)
                    if i == 2 and c > 0:
                        down_out(c - 1)
                down_out(NCH - 1)
            turn_vector(4)

        @block.tensor
        def _(pe):
            def turn_tensor(k):
                tn = turn[k]
                for u in range(NT // 2):
                    if u >= 4:
                        if k % 2 == 0:
                            pe.wait_ge(tn.moved_a, u - 3)
                        else:
                            pe.wait_ge(tn.moved_v, u - 3)
                    for t in range(2):
                        i = 2 * u + t
                        pe.wait_ge(tn.xhat, i + 1)
                        for kc in range(KC):
                            ins = pe.transpose(ps[:, u % 4, kc * 2 * P + t * P:kc * 2 * P + (t + 1) * P],
                                               A[:, i, kc * P:(kc + 1) * P], ident[:])
                    ins.then_inc(tn.tpose, 1)

            def mm(o, a, b, first, last):
                return pe.matmul(o, a, b, start=first, stop=last)

            def unit_products(L, u):
                p = proj[L]
                kind, m, c = UNITS[L][u]
                b = u % 4
                cs = slice(c * CH, (c + 1) * CH)
                if u >= 4:
                    pe.wait_ge(p.val, u - 3)
                if kind == "kr":
                    for kc in range(KC):
                        ins = mm(ps[:, b, :], w_kr[:, kc, :], XT[:, kc, cs], kc == 0, kc == KC - 1)
                elif kind == "q":
                    pe.wait_ge(p.zq_sb, c + 1)
                    pe.wait_ge(p.rot, 6)
                    ins = mm(ps[:, b, :], w_uq[:, m * P:(m + 1) * P], cq_t[0:DQ, cs], True, True)
                elif kind == "kn":
                    pe.wait_ge(p.zkv_sb, c + 1)
                    ins = mm(ps[:, b, :], w_kn, ckv_t[:, cs], True, True)
                else:
                    for kc in range(KC):
                        ins = mm(ps[:, b, :], w_qkv[:, kc, m * P:(m + 1) * P], XT[:, kc, cs], kc == 0, kc == KC - 1)
                ins.then_inc(p.u_ps, 1)

            def v_products(L, v):
                p = proj[L]
                if L == 0 and v == 0:
                    pe.wait_ge(p.zkv_sb, NCH)
                if v >= 2:
                    pe.wait_ge(p.v_sb, v - 1)
                for t in range(2):
                    ts = slice((2 * v + t) * P, (2 * v + t + 1) * P)
                    o = ps[:, 6 + v % 2, t * C:(t + 1) * C]
                    if L == 0:
                        if v < 2:
                            pe.wait_ge(p.zq_sb, NCH)
                        ins = mm(o, ckv_t[:, ts], w_v0, True, True)
                    else:
                        for kc in range(KC):
                            ins = mm(o, XT[:, kc, ts], w_qkv[:, kc, 2 * C:3 * C], kc == 0, kc == KC - 1)
                ins.then_inc(p.v_ps, 1)

            pe.wait_ge(ident_in, 16)
            pe.wait_ge(setup_done, 3)
            for L in range(2):
                p = proj[L]
                turn_tensor(2 * L)
                pe.wait_ge(turn[2 * L].moved_a, NT // 2)
                pe.wait_ge(w_in[L], 16 * (7 if L == 0 else 2))
                if L == 0:
                    for i in range(NT):
                        if i >= 2:
                            pe.wait_ge(p.down_sb, i - 1)
                        for kc in range(KC):
                            ins = mm(ps[:, 4 + i % 2, 0:DQ + DKV], XT[:, kc, i * P:(i + 1) * P], w_down[:, kc, :],
                                     kc == 0, kc == KC - 1)
                        ins.then_inc(p.down_ps, 1)
                    unit_products(0, 0)
                    pe.wait_ge(p.down_sb, NT)
                    for g in range(NCH):
                        if g >= 2:
                            pe.wait_ge(p.zq_sb, g - 1)
                            pe.wait_ge(p.zkv_sb, g - 1)
                        b = 4 + 2 * (g % 2)
                        for t in range(TPC):
                            i = TPC * g + t
                            pe.wait_ge(p.z, 2 * i + 2)
                            pe.transpose(ps[0:DQ, b, t * P:(t + 1) * P], c_down[:, i, 0:DQ], ident[:])
                            ins = pe.transpose(ps[:, b + 1, t * P:(t + 1) * P], c_down[:, i, DQ:DQ + DKV], ident[:])
                        ins.then_inc(p.zt_ps, 1)
                    first = 1
                else:
                    first = 0
                for u in range(first, NU):
                    unit_products(L, u)
                    for v in v_after(L, u):
                        v_products(L, v)

                if L == 0:
                    pe.wait_ge(consts_in, 48)
                    pe.wait_ge(ones_done, 1)
                pe.wait_ge(p.val, NU)
                pe.wait_ge(p.v_sb, VU)
                
                seen = set()
                n_half = 16 * 2 * len(STACK_RUNS)
                pe.wait_ge(stack_half[L], n_half)
                stepped = set()
                for o in ORDER:
                    if o.ring is not None and o.ring >= RING:
                        pe.wait_ge(s.ring_free, L * RING_N + o.ring - RING + 1)
                    if o.kind == "S":
                        if o.g not in seen and (o.g > 0 or o.Q >= NCH // 2):
                            seen.add(o.g)
                            pe.wait_ge(stack_in[L][o.g % 2], n_half * (HALF * (o.g // 2 + 1) - (o.g % 2 == 0)))
                        n = CH if o.c < o.Q else P * (o.r + 1)
                        bank = ps[:, RING0 + o.ring % RING, :]
                        ins = mm(bank[:, 0:n], q_stack[0:NSTACK, o.g % 2, o.Q // CPH, o.h, q_at(o) + o.r * P:q_at(o) + (o.r + 1) * P],
                                 k_stack[0:NSTACK, o.g % 2, o.c // CPH, o.h, o.c % CPH * CH:o.c % CPH * CH + n], True, o.c < o.Q)
                        if o.c == o.Q:
                            ins = mm(bank[:, n - P:n], ident_bf[:], causal[:], False, True)
                        ins.then_inc(s.ring_filled, 1)
                    if o.kind == "MT":
                        pe.wait_ge(s.mparts, 4 * (L * NSTEP + o.n + 1))
                        pe.transpose(ps[:, RING0 + o.ring % RING, 0:P // 2].bitcast(BF16),
                                     m_parts[:, o.n % 2, :], ident_bf[:]).then_inc(s.ring_filled, 1)
                    if o.kind == "T":
                        if o.n not in stepped:
                            stepped.add(o.n)
                            pe.wait_ge(mrows_in[o.n % 2], L * MROWS_N + 16 * HG * (o.n // 2 + 1))
                        if o.k >= 2:
                            pe.wait_ge(s.exp_done, L * T_N + o.k - 1)
                        for h in range(2):
                            hh = 2 * o.hp + h
                            ins = mm(psT[:, o.k % 2, h, o.off:CH],
                                     k_stack[0:KROWS, o.g % 2, o.kt // KPH, hh, o.kt % KPH * P:(o.kt % KPH + 1) * P],
                                     q_stack[0:KROWS, o.g % 2, o.Q // CPH, hh, q_at(o) + o.off:q_at(o) + CH], True, True)
                        ins.then_inc(s.t_filled, 1)
                    if o.kind == "PV":
                        if o.sel is not None:
                            pe.wait_ge(s.selected, L * SEL_N + o.sel)
                        else:
                            pe.wait_ge(s.exp_done, L * T_N + 2 * o.j + 2)
                        if o.first:
                            pe.wait_ge(s.v_staged, L * NG + o.g + 1)
                            if o.n == 0:
                                pe.wait_ge(s.v_ones, L + 1)
                            if o.n > 0:
                                pe.wait_ge(s.y_evac, L * NSTEP + o.n)
                        for h in range(HG):
                            ins = mm(ps[32 * h:32 * h + VW, PV_BANK, o.off:CH], v_stage[:, o.g % 2, o.kt, h, :],
                                     probs[:, o.j % SLOTS, h, o.off:CH], o.first, o.last)
                        ins.then_inc(s.pv_done, 1)
                    if o.kind == "YT":
                        pe.wait_ge(s.y_evac, L * NSTEP + o.n + 1)
                        for r in range(TPC):
                            ins = pe.transpose(ps[:, RING0 + o.ring % RING, r * P:(r + 1) * P],
                                               y_chunk[:, o.n % 2, r * P:(r + 1) * P], ident[:])
                        ins.then_inc(s.ring_filled, 1)
                pe.wait_ge(s.ring_free, (L + 1) * RING_N)
                pe.wait_ge(s.exp_done, (L + 1) * T_N)

                q = oproj[L]

                def o_transpose(u):
                    if u >= 2:
                        pe.wait_ge(q.yt_sb, u - 1)
                    for t in range(2):
                        for kc in range(KC):
                            ins = pe.transpose(ps[:, u % 2, (2 * t + kc) * P:(2 * t + kc + 1) * P],
                                               Y[:, 2 * u + t, kc * P:(kc + 1) * P], ident[:])
                    ins.then_inc(q.yt_ps, 1)

                o_transpose(0)
                for u in range(NT // 2):
                    if u + 1 < NT // 2:
                        o_transpose(u + 1)
                    pe.wait_ge(q.yt_sb, u + 1)
                    if u >= 2:
                        pe.wait_ge(q.o_sb, 2 * (u - 1))
                    for t in range(2):
                        for kc in range(KC):
                            ins = mm(ps[:, 2 + u % 2, t * C:(t + 1) * C], y_t[:, u % 2, 2 * t + kc, :], w_o[:, kc, :],
                                     kc == 0, kc == KC - 1)
                    ins.then_inc(q.o_ps, 1)

                turn_tensor(1 + 2 * L)
                f = ffn[L]
                pe.wait_ge(turn[1 + 2 * L].moved_v, NT // 2)
                pe.wait_ge(wffn_done[L], 3)

                def down(u):
                    c, i = divmod(u, NI)
                    pe.wait_ge(f.lo, u + 1)
                    if i == 0 and c > 0:
                        pe.wait_ge(f.evac, TPC * c)
                    for t in range(TPC):
                        for k, part in enumerate((fuse_hi, frem_hi, flo_r)):
                            ins = mm(ps[:, 4 + t, 0:C], part[:, u % 3, t * P:(t + 1) * P], w_dn[:, i, :],
                                     i == 0 and k == 0, i == NI - 1 and k == 2)
                    ins.then_inc(f.down, 1)

                for u in range(NCH * NI):
                    c, i = divmod(u, NI)
                    if u >= 2:
                        pe.wait_ge(f.fuse, u - 1)
                    for w, bank in ((w_gate, u % 2), (w_up, 2 + u % 2)):
                        for kc in range(KC):
                            for k in range(2):
                                ins = mm(ps[:, bank, :], w[:, kc, i * P:(i + 1) * P],
                                         x16[:, k, kc, c * CH:(c + 1) * CH], kc == 0 and k == 0,
                                         kc == KC - 1 and k == 1)
                    ins.then_inc(f.gu_ps, 1)
                    if u >= 2:
                        down(u - 2)
                down(NCH * NI - 2)
                down(NCH * NI - 1)


def kernel(**inputs):
    import concourse.bacc as bacc
    from concourse.bass_utils import run_bass_kernel_spmd

    w = {k: np.asarray(v) for k, v in inputs.items()}
    swap = np.arange(C).reshape(H, DH).copy()
    swap[:, DN:] = np.roll(swap[:, DN:], DR // 2, axis=1)
    swap = swap.reshape(-1)
    by_row = np.arange(C).reshape(2, H // 2, DH).transpose(0, 2, 1).reshape(-1)

    inv_freq = (np.float32(1.0 / 10000.0) ** (np.arange(0, DR, 2, dtype=np.float32) / np.float32(DR))).astype(np.float32)
    freqs = np.arange(H, dtype=np.float32)[:, None] * inv_freq[None, :]
    cos, sin = np.cos(freqs).astype(np.float32), np.sin(freqs).astype(np.float32)
    cos_row = np.concatenate([np.ones((H, DN), np.float32), cos, cos], axis=1).reshape(-1)
    sin_row = np.concatenate([np.zeros((H, DN), np.float32), sin, -sin], axis=1).reshape(-1)

    def tiles(a):
        return np.ascontiguousarray(a.reshape(-1, P, a.shape[1]).transpose(1, 0, 2))

    u_kv = w["L0_attn_W_u_kv"].reshape(H, DN + DH, DKV)
    b_ukv = w["L0_attn_b_u_kv"].reshape(H, DN + DH)
    cols = np.zeros((P, NCOLS), np.float32)
    cols[:DQ, 0], cols[:DQ, 1] = w["L0_attn_q_norm_g"], w["L0_attn_q_norm_b"]
    cols[:, 2], cols[:, 3] = w["L0_attn_kv_norm_g"], w["L0_attn_kv_norm_b"]
    cols[:, 4:6] = w["L0_attn_b_u_q"][by_row].reshape(2, P).T
    cols[:, 6:8] = w["L0_attn_b_u_q"][swap][by_row].reshape(2, P).T
    cols[:, 8] = b_ukv[:, :DN].T.reshape(-1)
    cols[:, 9] = np.repeat(w["L0_attn_b_d_kv"][DKV:], H)
    cos_row, sin_row = cos_row[by_row], sin_row[by_row]
    cols[:, 46:48], cols[:, 48:50] = cos_row.reshape(2, P).T, sin_row.reshape(2, P).T
    cols[:, 10:14] = w["L1_attn_b_qkv"][:2 * C].reshape(2, C)[:, by_row].reshape(4, P).T
    for L in range(2):
        cols[:, COLS["s_gate"][L]:COLS["s_gate"][L] + NI] = w[f"L{L}_ffn_s_gate"].reshape(NI, P).T
        cols[:, COLS["s_up"][L]:COLS["s_up"][L] + NI] = w[f"L{L}_ffn_s_up"].reshape(NI, P).T
    rows = np.concatenate([w["L0_attn_b_d_q"], w["L0_attn_b_d_kv"][:DKV], b_ukv[:, DN:].reshape(-1), w["L0_attn_b_o"],
                           w["L1_attn_b_qkv"][2 * C:], w["L1_attn_b_out"], w["L0_ffn_s_down"],
                           w["L1_ffn_s_down"], cos_row, sin_row]).reshape(1, NROWS)
    bf = mybir.dt.np(BF16)
    arrays = {
        "x": w["L0_attn_x"].reshape(T, C),
        "cols": cols, "rows": rows,
        "ident": np.eye(P, dtype=np.float32), "ident_bf": np.eye(P).astype(bf),
        "causal": np.triu(np.full((P, P), MASKED), 1).astype(bf),
        "w_down": tiles(np.concatenate([w["L0_attn_W_d_q"], w["L0_attn_W_d_kv"][:DKV]]).T),
        "w_kr": tiles(np.repeat(w["L0_attn_W_d_kv"][DKV:], H, axis=0).T),
        "w_uq": np.ascontiguousarray(w["L0_attn_W_u_q"][by_row].T),
        "w_uq_swap": np.ascontiguousarray(w["L0_attn_W_u_q"][swap][by_row].T),
        "w_kn": np.ascontiguousarray(u_kv[:, :DN].transpose(1, 0, 2).reshape(H * DN, DKV).T),
        "w_v0": np.ascontiguousarray(u_kv[:, DN:].reshape(H * DH, DKV).T),
        "w_qkv": tiles(w["L1_attn_w_qkv"][np.concatenate([by_row, C + by_row, np.arange(2 * C, 3 * C)])].T),
        "w_o": np.stack([tiles(w["L0_attn_W_o"].T), tiles(w["L1_attn_w_out"].T)]),
    }
    for name, key in (("w_gate", "w_gate"), ("w_up", "w_up"), ("w_dn", "w_down")):
        arrays[name] = np.stack([tiles(w[f"L{L}_ffn_{key}"]).reshape(P, -1) for L in range(2)]).view(np.int32)

    nc = bacc.Bacc("TRN2", target_bir_lowering=False, num_devices=1)
    D = {k: nc.dram_tensor(f"in_{k}", v.shape, mybir.dt.from_np(v.dtype), kind="ExternalInput").ap()
         for k, v in arrays.items()}
    for name, shape in (("q_parts", (2, HALF, 3, DH, H // 2, TH)), ("k_parts0", (HALF, 3, DH, H, TH)),
                        ("k_parts1", (2, HALF, 3, DH, H // 2, TH))):
        D[name] = nc.dram_tensor(name, shape, BF16, kind="Internal").ap()
    out = nc.dram_tensor("out_dram", (T, C), F32, kind="ExternalOutput").ap()
    build_program(nc, D, out)
    got = run_bass_kernel_spmd(nc, [{f"in_{k}": v for k, v in arrays.items()}], core_ids=[0])
    return got.results[0]["out_dram"].reshape(1, T, C)
```

```python
from contextlib import ExitStack
from collections import namedtuple

import numpy as np

import concourse.bass as bass
from concourse import mybir

ALU = mybir.AluOpType
ACT = mybir.ActivationFunctionType
AX = mybir.AxisListType
F32 = mybir.dt.float32
BF16 = mybir.dt.bfloat16
F16 = mybir.dt.float16
I8 = mybir.dt.int8

P = 128
T = 2048
C = 256
NT = T // P
KC = C // P
H = 16
DH = C // H
DQ = C // 3
DKV = C // 2
DN = DH // 2
DR = DH // 2
INTER = 1024
NI = INTER // P
EPS = 1e-5
CH = 512
NCH = T // CH
TPC = CH // P
HG = 4
NG = H // HG
Q_PARTS = (0, 0, 0, 1, 1, 2)
K_PARTS = (0, 1, 2, 0, 1, 0)
STACK_RUNS = ((0, 3), (3, 2), (5, 1))
HALF = 2
TH = T // HALF
CPH = NCH // HALF
NSTACK = DH * len(Q_PARTS)
NM = 3
KROWS = NSTACK + NM
VW = DH + 1
MASKED = -3.0e38
SCALE = 1.0 / DH ** 0.5

COLS = {"q_g": 0, "q_b": 1, "kv_g": 2, "kv_b": 3, "b_uq": 4, "b_uq_swap": 6, "b_kn": 8, "b_kr": 9,
        "b_qk1": 10, "s_gate": (14, 30), "s_up": (22, 38),
        "cos": 46, "sin": 48}
NCOLS = 50
ROWS = {"b_down": (0, DQ + DKV), "b_v": ((213, 256), (725, 256)), "b_o": ((469, 256), (981, 256)),
        "s_down": ((1237, 256), (1493, 256))}
NROWS = 1749

PB = 5
RING = 3
SLOTS = 3
PE_LAT, SEM_NS, DVE_NS, LOAD_NS = 160, 80, 70, 20000
STEP_ORDER = [(g, Q) for g in range(NG) for Q in (range(NCH) if g % 2 == 0 else reversed(range(NCH)))]
LEAD, LEAD_REST = 280, 4

Step = namedtuple("Step", "kind n g Q h r c kt off first last hp ring k j sel", defaults=(None,) * 14)


def plan_attention():
    steps = STEP_ORDER
    n_steps = len(steps)
    s_units = [(n, h, r, c) for n, (_, Q) in enumerate(steps) for h in range(HG) for r in range(TPC)
               for c in range(Q + 1)]
    kts = [list(range(TPC * Q, TPC * Q + TPC)) + list(range(TPC * Q)) for _, Q in steps]
    t_list = [(n, i, kt, hp) for n in range(n_steps) for i, kt in enumerate(kts[n]) for hp in range(2)]
    pv_list = [(n, i, kt) for n in range(n_steps) for i, kt in enumerate(kts[n])]
    size = [sum(HG * (TPC * Q + r + 1) for r in range(TPC)) for _, Q in steps]
    upto = [sum(size[:n]) for n in range(n_steps + 1)] + [sum(size)]
    s_done = t_done = 0
    order = []
    pe = dve = act = pool = 0.0
    ring_free = [0.0] * RING
    m_parts, m_rows, evac, exp_end, t_end = {}, {}, {}, {}, {}
    pair_free = [0.0] * 2
    v_free = 0.0
    ring = k = si = mt = yt = ti = pi = sel = sel_used = 0
    while yt < n_steps:
        cand = []
        if mt < n_steps and mt in m_parts:
            cand.append((0, max(m_parts[mt], ring_free[ring % RING]), "MT"))
        if yt in evac:
            cand.append((1, max(evac[yt], ring_free[ring % RING]), "YT"))
        if si < len(s_units) and s_units[si][0] < mt + 2:
            g = steps[s_units[si][0]][0]
            if g < 2 or g - 2 in t_end:
                n = t_list[ti][0] if ti < len(t_list) else n_steps - 1
                target = upto[n + 1] + (upto[n + 2] - upto[n + 1]) * (t_done - upto[n]) / size[n] + min(
                    LEAD, (upto[n_steps] - t_done) / LEAD_REST)
                cand.append((2 if s_done < target else 5, max(ring_free[ring % RING], t_end[g - 2] + LOAD_NS if g >= 2 else 0), "S"))
        if pi < len(pv_list) and pi in exp_end:
            n, i, kt = pv_list[pi]
            if i > 0 or n == 0 or n - 1 in evac:
                cand.append((4.5, max(exp_end[pi], v_free if i == 0 else 0), "PV"))
        if ti < len(t_list):
            n, i, kt, hp = t_list[ti]
            if n in m_rows and ti // 2 < pi + SLOTS:
                cand.append((4, max(m_rows[n], pair_free[k % 2]), "T"))
        ready_now = [x for x in cand if x[1] <= pe + 1]
        _, ready, kind = min(ready_now) if ready_now else min(cand, key=lambda x: (x[1], x[0]))
        pe = max(pe, ready)
        if kind == "S":
            n, h, r, c = s_units[si]
            g, Q = steps[n]
            width = CH if c < Q else P * (r + 1)
            pe += width / 2.4 + 6
            dve = max(dve, pe + PE_LAT) + width / 0.96 + DVE_NS
            ring_free[ring % RING] = dve + SEM_NS
            si += 1
            s_done += width // P
            last = si == len(s_units) or s_units[si][0] != n
            order.append(Step("S", n, g, Q, h=h, r=r, c=c, last=last, ring=ring))
            ring += 1
            if last:
                dve += 150
                pool = max(pool, dve + 100) + 900
                m_parts[n] = pool + 100
        elif kind == "MT":
            g, Q = steps[mt]
            pe += 70
            dve = max(dve, pe + PE_LAT) + 150
            ring_free[ring % RING] = dve + SEM_NS
            order.append(Step("MT", mt, g, Q, ring=ring))
            ring += 1
            m_rows[mt] = dve + 2800
            mt += 1
        elif kind == "YT":
            g, Q = steps[yt]
            pe += 300
            dve = max(dve, pe + PE_LAT) + 500
            ring_free[ring % RING] = dve + SEM_NS
            order.append(Step("YT", yt, g, Q, ring=ring))
            ring += 1
            yt += 1
        elif kind == "T":
            n, i, kt, hp = t_list[ti]
            g, Q = steps[n]
            diag = kt >= TPC * Q
            off = P * (kt - TPC * Q) if diag else 0
            pe += 2 * (CH - off) / 2.4 + 12
            t_done += 2 * (CH - off) // P
            act = max(act, pe + PE_LAT) + 2 * (CH - off) / 1.2 + 55
            pair_free[k % 2] = act + SEM_NS
            last = i == len(kts[n]) - 1 and hp == 1
            order.append(Step("T", n, g, Q, kt=kt, off=off, hp=hp, k=k, j=ti // 2, first=diag, last=last))
            k += 1
            if hp == 1:
                exp_end[ti // 2] = act + SEM_NS
                if diag:
                    pool = max(pool, act + 60) + 600
                    exp_end[ti // 2] = pool + SEM_NS
                    sel += 1
            if last and all(g2 != g for g2, _ in steps[n + 1:]):
                t_end[g] = pe
            ti += 1
        else:
            n, i, kt = pv_list[pi]
            g, Q = steps[n]
            diag = kt >= TPC * Q
            off = P * (kt - TPC * Q) if diag else 0
            sel_used += diag
            pe += 4 * (CH - off) / 2.4 * 1.08
            last = i == len(kts[n]) - 1
            order.append(Step("PV", n, g, Q, kt=kt, off=off, first=i == 0, last=last, j=pi,
                              sel=sel_used if diag else None))
            if last:
                act = max(act, pe + PE_LAT) + 480
                v_free = evac[n] = act + SEM_NS
            pi += 1
    return steps, order


def build_program(nc, D, out):
    STEPS, ORDER = plan_attention()
    NSTEP = len(STEPS)
    RING_N = sum(1 for o in ORDER if o.ring is not None)
    T_N = sum(1 for o in ORDER if o.kind == "T")
    PV_N = sum(1 for o in ORDER if o.kind == "PV")
    SEL_N = max(o.sel for o in ORDER if o.kind == "PV" and o.sel is not None)
    MT_RING = {o.n: o.ring for o in ORDER if o.kind == "MT"}
    YT_RING = {o.n: o.ring for o in ORDER if o.kind == "YT"}
    LAST_T = {o.g: o.k for o in ORDER if o.kind == "T"}
    LAST_PV = {o.g: o.j for o in ORDER if o.kind == "PV"}

    with ExitStack() as ctx:
        def sb(name, shape, dt):
            return ctx.enter_context(nc.sbuf_tensor(name, shape, dt))

        def sem(name):
            return ctx.enter_context(nc.semaphore(name))

        X = sb("X", [P, NT, C], F32)
        region_a = sb("region_a", [P, NT * C], F32)
        region_v = sb("region_v", [P, NT * C], F32)
        region_vst = sb("region_vst", [P, 2 * NT * HG * VW], F32)
        region_p = sb("region_p", [P, SLOTS * HG * CH], F32)
        q_stack = sb("q_stack", [P, 2, HALF, HG, TH], BF16)
        k_stack = sb("k_stack", [P, 2, HALF, HG, TH], BF16)
        w_attn = sb("w_attn", [P, 2090], F32)
        w_ffn = sb("w_ffn", [P, 3 * KC * INTER], BF16)
        w_raw = sb("w_raw", [P, 3 * KC * INTER], I8)
        cols = sb("cols", [P, NCOLS], F32)
        rows = sb("rows", [P, NROWS], F32)
        ident = sb("ident", [P, P], F32)
        zeros = sb("zeros", [1, P], BF16)
        ident_bf = sb("ident_bf", [P, P], BF16)
        causal = sb("causal", [P, CH], F32)
        rem = sb("rem", [P, 2, CH], F32)
        parts = sb("parts", [P, PB, 3, CH], BF16)
        y_chunk = sb("y_chunk", [P, 2, CH], F32)
        m_tile = sb("m_tile", [P, 2, HG * TPC, NCH], F32)
        neg_max = sb("neg_max", [P, 2, HG * TPC], F32)
        m_rem = sb("m_rem", [P, 2, HG * TPC], F32)
        m_parts = sb("m_parts", [P, 2, P], BF16)
        m_rows = sb("m_rows", [NM * HG * TPC, 2, P], BF16)
        recip = sb("recip", [P, TPC, HG], F32)
        stats = sb("stats", [P, NT, 2, 6], F32)
        mv = sb("mv", [P, NT, 2, 2], F32)
        std = sb("std", [P, NT, 2], F32)
        rstd = sb("rstd", [P, NT, 2], F32)
        eps = sb("eps", [P, 1], F32)
        ps = ctx.enter_context(nc.psum_tensor("ps", [P, 8, 512], F32))

        XT = region_a[:].rearrange("p (k t) -> p k t", k=KC)
        Y = region_a[:].rearrange("p (i c) -> p i c", i=NT)
        x16 = region_a[:].bitcast(F16).rearrange("p (s k t) -> p s k t", s=2, k=KC)
        V = region_v[:].rearrange("p (i c) -> p i c", i=NT)
        v_stage = region_vst[:].rearrange("p (b i h w) -> p b i h w", b=2, i=NT, h=HG)
        probs = region_p[:].rearrange("p (s h q) -> p s h q", s=SLOTS, h=HG)
        A = region_p[:, 0:NT * C].rearrange("p (i c) -> p i c", i=NT)
        c_down = region_p[:, 0:NT * (DQ + DKV)].rearrange("p (i c) -> p i c", i=NT)
        q_flat = q_stack[:].rearrange("p b s h t -> p (b s h t)").bitcast(F32)
        cq_t, ckv_t = (q_flat[:, i * T:(i + 1) * T] for i in (2, 3))
        y_t = q_flat[:, 0:2 * CH].rearrange("p (b k t) -> p b k t", b=2, k=KC * 2)
        gate_r = region_v[:, 0:2 * CH].rearrange("p (s t) -> p s t", s=2)
        fuse_r = region_v[:, 2 * CH:5 * CH].rearrange("p (s t) -> p s t", s=3)
        frem_r = region_v[:, 5 * CH:8 * CH].rearrange("p (s t) -> p s t", s=3)
        flo_r = region_vst[:, 0:3 * CH // 2].bitcast(BF16).rearrange("p (s t) -> p s t", s=3)
        fuse_hi = fuse_r.bitcast(BF16).rearrange("p s (t two) -> p s t two", two=2)[:, :, :, 1]
        frem_hi = frem_r.bitcast(BF16).rearrange("p s (t two) -> p s t two", two=2)[:, :, :, 1]
        rotary = y_chunk[:].rearrange("p b q -> p (b q)")[:, 0:2 * C]
        w_down = w_attn[:, 0:KC * 213].rearrange("p (k c) -> p k c", k=KC)
        w_kr = w_attn[:, 426:682].rearrange("p (k c) -> p k c", k=KC)
        w_uq = w_attn[0:DQ, 682:938]
        w_uq_swap = w_attn[0:DQ, 938:1194]
        w_kn = w_attn[:, 1194:1322]
        w_v0 = w_attn[:, 1322:1578]
        w_qkv = w_attn[:, 0:KC * 3 * C].rearrange("p (k c) -> p k c", k=KC)
        w_o = w_attn[:, 1578:2090].rearrange("p (k c) -> p k c", k=KC)
        w_gate, w_up = (w_ffn[:, i * KC * INTER:(i + 1) * KC * INTER].rearrange("p (k c) -> p k c", k=KC)
                        for i in range(2))
        w_dn = w_ffn[:, 2 * KC * INTER:].rearrange("p (k c) -> p k c", k=NI)
        psT = ps[:, 0:4, :].rearrange("p (b h) q -> p b h q", b=2)
        RING0, PV_BANK = 4, 7

        def col(name, width=1, n=P, layer=None, at=0):
            c = COLS[name] if layer is None else COLS[name][layer]
            return cols[0:n, c + at:c + at + width]

        def row(name, layer=None):
            a, n = ROWS[name] if layer is None else ROWS[name][layer]
            return rows[:, a:a + n]

        ident_in = sem("ident_in")
        consts_in = sem("consts_in")
        rows_in = sem("rows_in")
        x_in = [sem(f"x_in{i}") for i in range(4)]
        w_in = [sem(f"w_in{L}") for L in range(2)]
        wraw_in = [sem(f"wraw_in{L}") for L in range(2)]
        wffn_done = [sem(f"wffn_done{L}") for L in range(2)]
        setup_done = sem("setup_done")
        ones_done = sem("ones_done")
        out_stored = sem("out_stored")

        def Sems(stage, *names):
            return namedtuple(stage, names)(*[sem(f"{stage}_{n}") for n in names])

        TURN_IN = ("stats_done", "std_done", "rstd_done", "normed", "added")
        TURN_OUT = ("stats2", "var2", "std2", "rstd2", "xhat", "tpose", "moved_a", "moved_v")
        turn = [Sems(f"turn{k}", *(TURN_IN if k > 0 else ()), *(TURN_OUT if k < 4 else ())) for k in range(5)]
        SPLIT = ("u_ps", "hi", "rem", "mid", "lo", "v_ps", "v_sb")
        proj = [Sems("proj0", *SPLIT, "rot", "down_ps", "down_sb", "stat", "var", "std", "rstd", "z", "zt_ps", "zq_sb",
                     "zkv_sb"), Sems("proj1", *SPLIT)]
        parts_stored = [[sem(f"parts_stored{L}{b}") for b in range(PB)] for L in range(2)]
        stack_in = [[sem(f"stack{L}{b}") for b in range(2)] for L in range(2)]
        stack_half = [sem(f"stack_half{L}") for L in range(2)]
        s = Sems("att", "ring_filled", "ring_free", "negmax", "mparts", "t_filled", "exp_done", "selected",
                 "pv_done", "y_evac", "rcp", "v_staged", "v_ones")
        mrows_in = [sem(f"mrows_in{i}") for i in range(2)]
        MROWS_N = 16 * HG * (NSTEP // 2)
        oproj = [Sems(f"oproj{L}", "yt_ps", "yt_sb", "o_ps", "o_sb", "st") for L in range(2)]
        ffn = [Sems(f"ffn{L}", "gu_ps", "gate", "fuse", "rem", "lo", "down", "evac", "st") for L in range(2)]

        UNITS = [
            [(kind, 0, c) for c in range(NCH) for kind in ("kr", "q", "kn")] + [("q", 1, c) for c in range(NCH)],
            [("qk", m, c) for c in range(NCH) for m in (0, 2)] + [("qk", m, c) for c in range(NCH) for m in (1, 3)],
        ]
        NU = 16
        VU = NT // 2
        EARLY = (12, 8)

        def v_after(L, u):
            if u < EARLY[L]:
                return range(0)
            n = VU // (NU - EARLY[L])
            return range((u - EARLY[L]) * n, (u - EARLY[L] + 1) * n)
        def unit_dram(L, u):
            kind, m, c = UNITS[L][u]
            if kind == "qk":
                kind, m = ("q", m) if m < 2 else ("k", m - 2)
            half, ts = c // CPH, slice(c % CPH * CH, (c % CPH + 1) * CH)
            if kind in ("kn", "kr"):
                d = slice(0, DN) if kind == "kn" else slice(DN, DH)
                return D["k_parts0"][half, :, d, :, ts].rearrange("s d h t -> (d h) s t")
            return D["q_parts" if kind == "q" else "k_parts1"][m, half, :, :, :, ts].rearrange("s d h t -> (d h) s t")

        KPH = NT // HALF

        PE_BEFORE = {0: [("down", 0), ("down", 1)], 1: [("down", 2), ("zt", 0)], 3: [("down", 3)], 4: [("zt", 1)],
                     7: [("zt", 2)], 10: [("zt", 3)]}
        DVE_BEFORE = {0: [("down", 0), ("down", 1), ("z", 0)], 1: [("down", 2), ("c", 0), ("z", 1)],
                      3: [("down", 3)], 4: [("c", 1), ("z", 2)], 7: [("c", 2), ("z", 3)], 10: [("c", 3)]}
        ACT_BEFORE = {0: [("sqrt", 0), ("sqrt", 1)], 1: [("c", 0), ("sqrt", 2)], 3: [("sqrt", 3)], 4: [("c", 1)],
                      7: [("c", 2)], 10: [("c", 3)]}

        def unit_bias(L, u):
            kind, m, c = UNITS[L][u]
            return {"kr": col("b_kr"), "q": col("b_uq", at=m), "kn": col("b_kn"), "qk": col("b_qk1", at=m)}[kind]

        def before(L, plan, u):
            return plan.get(u, []) if L == 0 else []

        XHAT_AT = (4, 3, 3, NI)

        def t_bank(k, u):
            return (0, 1, 2, 3, 6, 7, 4, 5)[u] if k % 2 == 0 else 6 + u % 2

        def q_at(o):
            return o.Q % CPH * CH

        block = ctx.enter_context(nc.Block())

        @block.sync
        def _(sp):
            xin = D["x"].rearrange("(i p) c -> p i c", p=P)
            for g in range(4):
                sp.dma_start(X[:, 4 * g:4 * g + 4, :], xin[:, 4 * g:4 * g + 4, :]).then_inc(x_in[g], 16)

            for L in range(2):
                def stack_dmas(g, halves=range(HALF)):
                    dmas = []
                    h0 = g % 2 * HG
                    for half in halves:
                        for first, n in STACK_RUNS:
                            rows_ = slice(first * DH, (first + n) * DH)
                            part = Q_PARTS[first]
                            src = D["q_parts"][g // 2, half, part:part + 1, :, h0:h0 + HG, :]
                            dmas.append((q_stack[rows_, g % 2, half, :, :].rearrange("p h t -> p (h t)"),
                                         src.rearrange("s d h t -> s d (h t)").broadcast_to([n, DH, HG * TH])))
                            src = (D["k_parts0"][half, 0:n, :, g * HG:(g + 1) * HG, :] if L == 0 else
                                   D["k_parts1"][g // 2, half, 0:n, :, h0:h0 + HG, :])
                            dmas.append((k_stack[rows_, g % 2, half, :, :].rearrange("p h t -> p (h t)"),
                                         src.rearrange("s d h t -> s d (h t)")))
                    return dmas

                def load(b, dma, done=None):
                    sp.dma_start(dma[0], dma[1]).then_inc(done or stack_in[L][b], 16)

                def parts_complete(n):
                    for b in range(PB):
                        sp.wait_ge(parts_stored[L][b], 16 * ((n - b + PB - 1) // PB))

                for u in range(NU):
                    sp.wait_ge(proj[L].lo, u + 1)
                    sp.dma_start(unit_dram(L, u), parts[:, u % PB, :, :]).then_inc(parts_stored[L][u % PB], 16)
                    for half in range(HALF):
                        n = EARLY[L] * (half + 1) // HALF
                        if u == n + 1:
                            parts_complete(n)
                            for dma in stack_dmas(0, (half,)):
                                load(0, dma, stack_half[L] if half == 0 else None)
                parts_complete(NU)
                if L == 0:
                    sp.wait_ge(proj[L].v_ps, VU)
                queue = [(1, dma) for dma in stack_dmas(1)]
                for o in ORDER:
                    if o.kind == "MT":
                        sp.wait_ge(s.ring_free, L * RING_N + o.ring + 1)
                        for h in range(HG):
                            dst = q_stack[NSTACK:KROWS, o.g % 2, o.Q // CPH, h, q_at(o):q_at(o) + CH].rearrange(
                                "m (r t) -> m r t", r=TPC)
                            src = m_rows[h * NM * TPC:(h + 1) * NM * TPC, o.n % 2, :]
                            sp.dma_start(dst, src).then_inc(mrows_in[o.n % 2], 16)
                    if o.kind == "T" and o.k == LAST_T[o.g] and o.g + 2 < NG:
                        sp.wait_ge(s.t_filled, L * T_N + o.k + 1)
                        queue = [(o.g % 2, dma) for dma in stack_dmas(o.g + 2)]
                    elif queue and o.kind == "T":
                        load(*queue.pop(0))

            for g in range(4):
                sp.wait_ge(turn[4].added, 4 * g + 4)
                sp.dma_start(out.rearrange("(i p) c -> p i c", p=P)[:, 4 * g:4 * g + 4, :],
                             X[:, 4 * g:4 * g + 4, :]).then_inc(out_stored, 16)
            sp.wait_ge(out_stored, 64)

        @block.gpsimd
        def _(pool):
            def load_weights(L):
                if L == 0:
                    pool.dma_start(w_down, D["w_down"]).then_inc(w_in[0], 16)
                    pool.dma_start(w_kr, D["w_kr"]).then_inc(w_in[0], 16)
                    pool.dma_start(w_uq, D["w_uq"]).then_inc(w_in[0], 16)
                    pool.dma_start(w_uq_swap, D["w_uq_swap"]).then_inc(w_in[0], 16)
                    pool.dma_start(w_kn, D["w_kn"]).then_inc(w_in[0], 16)
                    pool.dma_start(w_v0, D["w_v0"]).then_inc(w_in[0], 16)
                else:
                    pool.wait_ge(oproj[0].o_ps, NT // 2)
                    pool.dma_start(w_qkv, D["w_qkv"]).then_inc(w_in[1], 16)
                pool.dma_start(w_o, D["w_o"][L]).then_inc(w_in[L], 16)

            def load_ffn(L):
                if L == 1:
                    pool.wait_ge(wffn_done[0], 3)
                raw = w_raw[:].bitcast(mybir.dt.int32).rearrange("p (s c) -> p s c", s=3)
                for s, name in enumerate(("w_gate", "w_up", "w_dn")):
                    pool.dma_start(raw[:, s, :], D[name][L]).then_inc(wraw_in[L], 16)

            pool.wait_ge(x_in[1], 16)
            pool.dma_start(rows[:], D["rows"].broadcast_to([P, NROWS])).then_inc(rows_in, 16)
            pool.dma_start(rotary, D["rotary"].broadcast_to([P, 2 * C])).then_inc(rows_in, 16)
            load_weights(0)
            load_ffn(0)
            nc.gpsimd.memset(k_stack[NSTACK:KROWS, :, :, :, :], 1.0).then_inc(ones_done, 1)
            pool.wait_ge(ones_done, 1)

            def split_lo(L, u):
                pool.wait_ge(proj[L].mid, u + 1)
                nc.gpsimd.tensor_tensor(parts[:, u % PB, 2, :], rem[:, u % 2, :], parts[:, u % PB, 1, :],
                                        ALU.subtract).then_inc(proj[L].lo, 1)

            def add_residual(k, i):
                pool.wait_ge(turn[k].normed, i + 1)
                nc.gpsimd.tensor_tensor(X[:, i, :], X[:, i, :], A[:, i, :], ALU.add).then_inc(turn[k].added, 1)

            def stage_ones(L):
                nc.gpsimd.memset(v_stage[:, :, :, :, DH:VW], 1.0).then_inc(s.v_ones, 1)

            for L in range(2):
                if L == 0:
                    stage_ones(0)
                for u in range(NU):
                    split_lo(L, u)
                pool.wait_ge(proj[L].v_sb, VU)
                if L == 1:
                    stage_ones(1)

                def stage_values(g):
                    nc.gpsimd.tensor_copy(v_stage[:, g % 2, :, :, 0:DH],
                                          V[:, :, g * HG * DH:(g + 1) * HG * DH].rearrange("p i (h d) -> p i h d", h=HG)
                                          ).then_inc(s.v_staged, 1)

                stage_values(0)
                stage_values(1)
                for o in ORDER:
                    if o.kind == "S" and o.last:
                        nm, mr = (m[:, o.n % 2, :].rearrange("p (h r) -> p h r", h=HG) for m in (neg_max, m_rem))
                        mp = m_parts[:, o.n % 2, 0:NM * HG * TPC].rearrange("p (h s r) -> p s h r", s=NM, h=HG)
                        c0 = 4 * (L * NSTEP + o.n)
                        pool.wait_ge(s.negmax, L * NSTEP + o.n + 1)
                        if o.n >= 2:
                            pool.wait_ge(s.ring_filled, L * RING_N + MT_RING[o.n - 2] + 1)
                        nc.gpsimd.tensor_copy(mp[:, 0, :, :], nm).then_inc(s.mparts, 1)
                        pool.wait_ge(s.mparts, c0 + 1)
                        nc.gpsimd.tensor_tensor(mr, nm, mp[:, 0, :, :], ALU.subtract).then_inc(s.mparts, 1)
                        pool.wait_ge(s.mparts, c0 + 2)
                        nc.gpsimd.tensor_copy(mp[:, 1, :, :], mr).then_inc(s.mparts, 1)
                        pool.wait_ge(s.mparts, c0 + 3)
                        nc.gpsimd.tensor_tensor(mp[:, 2, :, :], mr, mp[:, 1, :, :], ALU.subtract).then_inc(s.mparts, 1)
                    if o.kind == "T" and o.first and o.hp == 1:
                        pool.wait_ge(s.exp_done, L * T_N + o.k + 1)
                        blk = probs[:, o.j % SLOTS, :, o.off:o.off + P]
                        nc.gpsimd.affine_select(out=blk, in_=blk, compare_op=ALU.is_ge, fill=0.0, base=0,
                                                pattern=[[0, HG], [1, P]], channel_multiplier=-1
                                                ).then_inc(s.selected, 1)
                    if o.kind == "PV" and o.j == LAST_PV[o.g] and o.g + 2 < NG:
                        pool.wait_ge(s.pv_done, L * PV_N + o.j + 1)
                        stage_values(o.g + 2)
                for i in range(NT):
                    add_residual(1 + 2 * L, i)
                if L == 0:
                    load_weights(1)
                for u in range(NCH * NI):
                    c, i = divmod(u, NI)
                    pool.wait_ge(ffn[L].rem, u + 1)
                    if u >= 3:
                        pool.wait_ge(ffn[L].down, u - 2)
                    nc.gpsimd.tensor_tensor(flo_r[:, u % 3, :], frem_r[:, u % 3, :], frem_hi[:, u % 3, :],
                                            ALU.subtract).then_inc(ffn[L].lo, 1)
                    if i in (4, 5) and c > 0:
                        for t in range(2):
                            add_residual(2 + 2 * L, TPC * (c - 1) + 2 * (i - 4) + t)
                if L == 0:
                    load_ffn(1)

        @block.scalar
        def _(act):
            def sqrt_branch(k, b):
                act.wait_ge(turn[k].stats_done, TPC * (b + 1))
                nc.scalar.activation(std[:, TPC * b:TPC * (b + 1), 0], mv[:, TPC * b:TPC * (b + 1), 0, 1], ACT.Sqrt,
                                     bias=eps[:]).then_inc(turn[k].std_done, 1)

            def sqrt_residual(k, b):
                act.wait_ge(turn[k].stats2, TPC * (b + 1))
                nc.scalar.activation(std[:, TPC * b:TPC * (b + 1), 1], mv[:, TPC * b:TPC * (b + 1), 1, 1], ACT.Sqrt,
                                     bias=eps[:]).then_inc(turn[k].std2, 1)

            def move_transposed(k, b):
                for u in range(2 * b, 2 * b + 2):
                    act.wait_ge(turn[k].tpose, u + 1)
                    src = ps[:, t_bank(k, u), :].rearrange("p (k t) -> p k t", k=KC)
                    if k % 2 == 0:
                        nc.scalar.copy(XT[:, :, u * 2 * P:(u + 1) * 2 * P], src).then_inc(turn[k].moved_a, 1)
                    else:
                        nc.scalar.copy(x16[:, 0, :, u * 2 * P:(u + 1) * 2 * P], src).then_inc(turn[k].moved_a, 1)

            def convert_ffn(L):
                act.wait_ge(wraw_in[L], 48)
                if L == 1:
                    act.wait_ge(ffn[0].down, NCH * NI)
                n = KC * INTER
                for k in range(3):
                    nc.scalar.copy(w_ffn[:, k * n:(k + 1) * n], w_raw[:, k * n:(k + 1) * n]).then_inc(wffn_done[L], 1)

            def split_hi(L, u):
                act.wait_ge(proj[L].u_ps, u + 1)
                if u >= PB:
                    act.wait_ge(parts_stored[L][u % PB], 16 * (u // PB))
                nc.scalar.activation(parts[:, u % PB, 0, :], ps[:, u % 4, :], ACT.Identity,
                                     bias=unit_bias(L, u)).then_inc(proj[L].hi, 1)

            def split_mid(L, u):
                act.wait_ge(proj[L].rem, u + 1)
                nc.scalar.copy(parts[:, u % PB, 1, :], rem[:, u % 2, :]).then_inc(proj[L].mid, 1)

            act.dma_start(ident[:], D["ident"]).then_inc(ident_in, 16)
            act.dma_start(cols[:], D["cols"]).then_inc(consts_in, 16)
            act.dma_start(ident_bf[:], D["ident_bf"]).then_inc(consts_in, 16)
            act.dma_start(causal[:], D["causal"]).then_inc(consts_in, 16)
            act.wait_ge(setup_done, 4)
            act.wait_ge(consts_in, 48)
            for L in range(2):
                if L == 0:
                    for b in range(NCH):
                        sqrt_residual(0, b)
                        if b > 0:
                            move_transposed(0, b - 1)
                else:
                    for b in range(NCH - 1):
                        move_transposed(2, b)
                    sqrt_residual(2, NCH - 1)
                move_transposed(2 * L, NCH - 1)
                def chunk_scalar(what, c):
                    p = proj[0]
                    if what == "sqrt":
                        act.wait_ge(p.stat, 2 * TPC * (c + 1))
                        bs = slice(TPC * c, TPC * (c + 1))
                        nc.scalar.activation(std[:, bs, :], mv[:, bs, :, 1], ACT.Sqrt, bias=eps[:]).then_inc(p.std, 1)
                    else:
                        act.wait_ge(p.zt_ps, c + 1)
                        nc.scalar.activation(cq_t[0:DQ, c * CH:(c + 1) * CH], ps[0:DQ, 6, :], ACT.Identity,
                                             scale=col("q_g", n=DQ), bias=col("q_b", n=DQ)).then_inc(p.zq_sb, 1)

                for u in range(NU):
                    for what, c in before(L, ACT_BEFORE, u):
                        chunk_scalar(what, c)
                    split_hi(L, u)
                    if u > 0:
                        split_mid(L, u - 1)
                split_mid(L, NU - 1)
                convert_ffn(L)

                for o in ORDER:
                    if o.kind == "T":
                        act.wait_ge(s.t_filled, L * T_N + o.k + 1)
                        if o.j >= SLOTS:
                            act.wait_ge(s.pv_done, L * PV_N + o.j - SLOTS + 1)
                        nc.scalar.activation(probs[:, o.j % SLOTS, 2 * o.hp:2 * o.hp + 2, o.off:CH],
                                             psT[:, o.k % 2, :, o.off:CH], ACT.Exp, scale=SCALE).then_inc(s.exp_done, 1)
                    if o.kind == "PV" and o.last:
                        act.wait_ge(s.pv_done, L * PV_N + o.j + 1)
                        if o.n >= 2:
                            act.wait_ge(s.ring_filled, L * RING_N + YT_RING[o.n - 2] + 1)
                        nc.scalar.copy(y_chunk[:, o.n % 2, :], ps[:, PV_BANK, :]).then_inc(s.y_evac, 1)

                def o_move(u):
                    act.wait_ge(oproj[L].yt_ps, u + 1)
                    if u >= 2:
                        act.wait_ge(oproj[L].o_ps, u - 1)
                    nc.scalar.copy(y_t[:, u % 2, :, :], ps[:, u % 2, :].rearrange("p (k t) -> p k t", t=P)
                                   ).then_inc(oproj[L].yt_sb, 1)

                k1, k2 = 1 + 2 * L, 2 + 2 * L
                for u in range(4):
                    o_move(u)
                sqrt_branch(k1, 0)
                o_move(4)
                o_move(5)
                sqrt_branch(k1, 1)
                o_move(6)
                o_move(7)
                sqrt_branch(k1, 2)
                sqrt_residual(k1, 0)
                sqrt_branch(k1, 3)
                move_transposed(k1, 0)
                f = ffn[L]
                for u in range(NCH * NI):
                    c, i = divmod(u, NI)
                    act.wait_ge(f.gu_ps, u + 1)
                    if u >= 2:
                        act.wait_ge(f.fuse, u - 1)
                    nc.scalar.activation(gate_r[:, u % 2, :], ps[:, u % 2, :], ACT.Silu,
                                         scale=col("s_gate", layer=L, at=i)).then_inc(f.gate, 1)
                    if i == 3 and c > 0:
                        if k2 < 4 and c > 1:
                            sqrt_residual(k2, c - 2)
                        sqrt_branch(k2, c - 1)
                    if i == 3 and c == 0:
                        for b in range(1, NCH):
                            sqrt_residual(k1, b)
                    if i == XHAT_AT[c] + 2:
                        move_transposed(k1, c + 1)
                if k2 < 4:
                    sqrt_residual(k2, NCH - 2)
                sqrt_branch(k2, NCH - 1)

        @block.vector
        def _(dve):
            def stats_of(tiles, b, which, after, done, ready=None):
                batch = range(TPC * b, TPC * (b + 1))
                for i in batch:
                    if ready is not None:
                        dve.wait_ge(ready, i + 1)
                    nc.vector.bn_stats(stats[:, i, which, :], tiles[:, i, :]).then_inc(after, 1)
                for i in batch:
                    dve.wait_ge(after, i + 1)
                    nc.vector.bn_aggr(mv[:, i, which, :], stats[:, i, which, :]).then_inc(done, 1)

            def normalize_branch(k, b):
                tn = turn[k]
                bs = slice(TPC * b, TPC * (b + 1))
                dve.wait_ge(tn.std_done, b + 1)
                nc.vector.reciprocal(rstd[:, bs, 0], std[:, bs, 0]).then_inc(tn.rstd_done, 1)
                dve.wait_ge(tn.rstd_done, b + 1)
                for i in range(TPC * b, TPC * (b + 1)):
                    nc.vector.tensor_scalar(A[:, i, :], A[:, i, :], mv[:, i, 0, 0:1], rstd[:, i, 0:1], ALU.subtract,
                                            ALU.mult).then_inc(tn.normed, 1)

            def stats_residual(k, b):
                if k == 0:
                    dve.wait_ge(x_in[b], 16)
                stats_of(X, b, 1, turn[k].var2, turn[k].stats2, turn[k].added if k > 0 else None)

            def add_last(k):
                for i in range(TPC * (NCH - 1), NT):
                    dve.wait_ge(turn[k].normed, i + 1)
                    if i == TPC * (NCH - 1):
                        dve.wait_ge(turn[k].added, i)
                    nc.vector.tensor_tensor(X[:, i, :], X[:, i, :], A[:, i, :], ALU.add).then_inc(turn[k].added, 1)

            def normalize_residual(k, b):
                tn = turn[k]
                bs = slice(TPC * b, TPC * (b + 1))
                dve.wait_ge(tn.std2, b + 1)
                nc.vector.reciprocal(rstd[:, bs, 1], std[:, bs, 1]).then_inc(tn.rstd2, 1)
                dve.wait_ge(tn.rstd2, b + 1)
                for i in range(TPC * b, TPC * (b + 1)):
                    nc.vector.tensor_scalar(A[:, i, :], X[:, i, :], mv[:, i, 1, 0:1], rstd[:, i, 1:2], ALU.subtract,
                                            ALU.mult).then_inc(tn.xhat, 1)

            def low_parts(k, b):
                for u in range(2 * b, 2 * b + 2):
                    dve.wait_ge(turn[k].moved_a, u + 1)
                    sl = slice(u * 2 * P, (u + 1) * 2 * P)
                    nc.vector.tensor_tensor(x16[:, 1, :, sl], ps[:, t_bank(k, u), :].rearrange("p (k t) -> p k t", k=KC),
                                            x16[:, 0, :, sl], ALU.subtract).then_inc(turn[k].moved_v, 1)

            def unit_rem(L, u):
                p = proj[L]
                dve.wait_ge(p.hi, u + 1)
                if u >= 2:
                    dve.wait_ge(p.lo, u - 1)
                nc.vector.scalar_tensor_tensor(rem[:, u % 2, :], ps[:, u % 4, :], unit_bias(L, u), parts[:, u % PB, 0, :],
                                               ALU.add, ALU.subtract).then_inc(p.rem, 1)

            def v_value(L, v):
                dve.wait_ge(proj[L].v_ps, v + 1)
                for t in range(2):
                    ins = nc.vector.tensor_tensor(V[:, 2 * v + t, :], ps[:, 6 + v % 2, t * C:(t + 1) * C],
                                                  row("b_v", L), ALU.add)
                ins.then_inc(proj[L].v_sb, 1)

            nc.vector.memset(m_parts[:], 0.0).then_inc(setup_done, 1)
            nc.vector.memset(eps[:], EPS).then_inc(setup_done, 1)
            nc.vector.memset(zeros[:], 0.0).then_inc(setup_done, 1)
            nc.vector.memset(ps[:, PV_BANK, :], 0.0).then_inc(setup_done, 1)
            for L in range(2):
                p = proj[L]
                if L == 0:
                    for b in range(NCH):
                        stats_residual(0, b)
                        if b > 0:
                            normalize_residual(0, b - 1)
                else:
                    normalize_residual(2, NCH - 2)
                    normalize_branch(2, NCH - 1)
                    add_last(2)
                    stats_residual(2, NCH - 1)
                normalize_residual(2 * L, NCH - 1)
                if L == 0:
                    dve.wait_ge(consts_in, 48)
                    dve.wait_ge(rows_in, 32)
                    dve.wait_ge(w_in[0], 16 * 7)
                    for a, r in ((w_uq, rotary[0:DQ, 0:C]), (w_uq_swap, rotary[0:DQ, C:2 * C])):
                        nc.vector.tensor_tensor(a, a, r, ALU.mult).then_inc(p.rot, 1)
                    for a, name in (("b_uq", "cos"), ("b_uq_swap", "sin")):
                        nc.vector.tensor_tensor(col(a, 2), col(a, 2), col(name, 2), ALU.mult).then_inc(p.rot, 1)
                    dve.wait_ge(p.rot, 4)
                    nc.vector.tensor_tensor(w_uq, w_uq, w_uq_swap, ALU.add).then_inc(p.rot, 1)
                    nc.vector.tensor_tensor(col("b_uq", 2), col("b_uq", 2), col("b_uq_swap", 2), ALU.add
                                            ).then_inc(p.rot, 1)
                    dve.wait_ge(p.rot, 6)

                    dve.wait_ge(turn[0].tpose, NT // 2)
                    halves = tuple(enumerate((slice(0, DQ), slice(DQ, DQ + DKV))))

                    def chunk_down(c):
                        first, end = TPC * c, TPC * (c + 1)
                        for i in range(first, end + 2):
                            if i < end:
                                dve.wait_ge(p.down_ps, i + 1)
                                nc.vector.tensor_tensor(c_down[:, i, :], ps[:, 4 + i % 2, 0:DQ + DKV], row("b_down"),
                                                        ALU.add).then_inc(p.down_sb, 1)
                            if first <= i - 1 < end:
                                dve.wait_ge(p.down_sb, i)
                                for w, cs in halves:
                                    nc.vector.bn_stats(stats[:, i - 1, w, :], c_down[:, i - 1, cs]).then_inc(p.var, 1)
                            if first <= i - 2:
                                dve.wait_ge(p.var, 2 * (i - 1))
                                for w in range(2):
                                    nc.vector.bn_aggr(mv[:, i - 2, w, :], stats[:, i - 2, w, :]).then_inc(p.stat, 1)

                    def chunk_z(c):
                        bs = slice(TPC * c, TPC * (c + 1))
                        dve.wait_ge(p.std, c + 1)
                        nc.vector.reciprocal(rstd[:, bs, :], std[:, bs, :]).then_inc(p.rstd, 1)
                        dve.wait_ge(p.rstd, c + 1)
                        for i in range(TPC * c, TPC * (c + 1)):
                            for w, cs in halves:
                                nc.vector.tensor_scalar(c_down[:, i, cs], c_down[:, i, cs], mv[:, i, w, 0:1],
                                                        rstd[:, i, w:w + 1], ALU.subtract, ALU.mult).then_inc(p.z, 1)

                    def chunk_ckv(c):
                        dve.wait_ge(p.zt_ps, c + 1)
                        nc.vector.tensor_scalar(ckv_t[:, c * CH:(c + 1) * CH], ps[:, 7, :], col("kv_g"),
                                                col("kv_b"), ALU.mult, ALU.add).then_inc(p.zkv_sb, 1)

                    chunk = {"down": chunk_down, "z": chunk_z, "c": chunk_ckv}
                for u in range(NU):
                    for what, c in before(L, DVE_BEFORE, u):
                        chunk[what](c)
                    unit_rem(L, u)
                    for v in v_after(L, u):
                        v_value(L, v)

                base = L * RING_N
                for o in ORDER:
                    if o.kind == "S":
                        n = CH if o.c < o.Q else P * (o.r + 1)
                        if o.h == o.r == o.c == 0 and o.n >= 2:
                            dve.wait_ge(s.negmax, L * NSTEP + o.n - 1)
                        dve.wait_ge(s.ring_filled, base + o.ring + 1)
                        scores = ps[:, RING0 + o.ring % RING, 0:n]
                        maximum = m_tile[:, o.n % 2, o.h * TPC + o.r, o.c:o.c + 1]
                        if o.c < o.Q:
                            nc.vector.tensor_reduce(maximum, scores, AX.X, ALU.max).then_inc(s.ring_free, 1)
                        else:
                            nc.vector.tensor_tensor_reduce(scores, scores, causal[:, CH - n:CH], 1.0, MASKED, ALU.add,
                                                           ALU.max, maximum).then_inc(s.ring_free, 1)
                        if o.last:
                            dve.wait_ge(s.ring_free, base + o.ring + 1)
                            if o.n >= 2:
                                dve.wait_ge(s.mparts, 4 * (L * NSTEP + o.n - 1))
                            nc.vector.tensor_reduce(neg_max[:, o.n % 2, :], m_tile[:, o.n % 2, :, 0:o.Q + 1], AX.X,
                                                    ALU.max, negate=True).then_inc(s.negmax, 1)
                    if o.kind == "MT":
                        dve.wait_ge(s.ring_filled, base + o.ring + 1)
                        if o.n >= 2:
                            dve.wait_ge(mrows_in[o.n % 2], L * MROWS_N + 16 * HG * (o.n // 2))
                        src = ps[0:NM * HG * TPC, RING0 + o.ring % RING, 0:P // 2].bitcast(BF16)
                        nc.vector.tensor_copy(m_rows[:, o.n % 2, :], src).then_inc(s.ring_free, 1)
                    if o.kind == "YT":
                        dve.wait_ge(s.ring_filled, base + o.ring + 1)
                        y4 = ps[:, RING0 + o.ring % RING, :].rearrange("p (r h w) -> p r h w", r=TPC, h=HG)
                        if o.n >= 1:
                            dve.wait_ge(s.ring_free, base + YT_RING[o.n - 1] + 1)
                        nc.vector.reciprocal(recip[:], y4[:, :, :, DH]).then_inc(s.rcp, 1)
                        dve.wait_ge(s.rcp, L * NSTEP + o.n + 1)
                        dst = Y[:, TPC * o.Q:TPC * (o.Q + 1), o.g * HG * DH:(o.g + 1) * HG * DH]
                        nc.vector.tensor_tensor(dst.rearrange("p r (h d) -> p r h d", h=HG), y4[:, :, :, 0:DH],
                                                recip[:].rearrange("p r (h o) -> p r h o", o=1)
                                                .broadcast_to([P, TPC, HG, DH]), ALU.mult).then_inc(s.ring_free, 1)

                q = oproj[L]
                k1, k2 = 1 + 2 * L, 2 + 2 * L

                def o_value(b):
                    for i in range(TPC * b, TPC * (b + 1)):
                        if i % 2 == 0:
                            dve.wait_ge(q.o_ps, i // 2 + 1)
                        nc.vector.tensor_tensor(A[:, i, :], ps[:, 2 + i // 2 % 2, i % 2 * C:(i % 2 + 1) * C],
                                                row("b_o", L), ALU.add).then_inc(q.o_sb, 1)
                    stats_of(A, b, 0, q.st, turn[k1].stats_done, q.o_sb)

                o_value(0)
                o_value(1)
                normalize_branch(k1, 0)
                o_value(2)
                stats_residual(k1, 0)
                normalize_branch(k1, 1)
                o_value(3)
                normalize_residual(k1, 0)
                normalize_branch(k1, 2)
                low_parts(k1, 0)
                normalize_branch(k1, 3)
                f = ffn[L]

                def down_out(c):
                    dve.wait_ge(f.down, NI * (c + 1))
                    for t in range(TPC):
                        i = TPC * c + t
                        nc.vector.tensor_tensor(A[:, i, :], ps[:, 4 + t // 2, t % 2 * C:(t % 2 + 1) * C], row("s_down", L),
                                                ALU.mult).then_inc(f.evac, 1)
                    stats_of(A, c, 0, f.st, turn[2 + 2 * L].stats_done, f.evac)

                for u in range(NCH * NI):
                    c, i = divmod(u, NI)
                    dve.wait_ge(f.gate, u + 1)
                    if u >= 3:
                        dve.wait_ge(f.down, u - 2)
                    nc.vector.scalar_tensor_tensor(fuse_r[:, u % 3, :], ps[:, 2 + u % 2, :], col("s_up", layer=L, at=i),
                                                   gate_r[:, u % 2, :], ALU.mult, ALU.mult).then_inc(f.fuse, 1)
                    dve.wait_ge(f.fuse, u + 1)
                    nc.vector.tensor_tensor(frem_r[:, u % 3, :], fuse_r[:, u % 3, :], fuse_hi[:, u % 3, :],
                                            ALU.subtract).then_inc(f.rem, 1)
                    if i == 1 and c > 0:
                        down_out(c - 1)
                    if c == 0 and i < 3:
                        stats_residual(k1, i + 1)
                    if i == XHAT_AT[c]:
                        normalize_residual(k1, c + 1)
                    if i == XHAT_AT[c] + 2:
                        low_parts(k1, c + 1)
                    if i == 4 and c > 0:
                        normalize_branch(k2, c - 1)
                        if k2 < 4 and c > 1:
                            normalize_residual(k2, c - 2)
                    if i == 7 and c > 0 and k2 < 4:
                        stats_residual(k2, c - 1)
                down_out(NCH - 1)
            normalize_branch(4, NCH - 1)
            add_last(4)

        @block.tensor
        def _(pe):
            def transpose_batch(k, b):
                for u in range(2 * b, 2 * b + 2):
                    if k % 2 == 1 and u >= 2:
                        pe.wait_ge(turn[k].moved_v, u - 1)
                    for t in range(2):
                        i = 2 * u + t
                        pe.wait_ge(turn[k].xhat, i + 1)
                        for kc in range(KC):
                            ins = pe.transpose(ps[:, t_bank(k, u), kc * 2 * P + t * P:kc * 2 * P + (t + 1) * P],
                                               A[:, i, kc * P:(kc + 1) * P], ident[:])
                    ins.then_inc(turn[k].tpose, 1)

            def mm(o, a, b, first, last):
                return pe.matmul(o, a, b, start=first, stop=last)

            def unit_products(L, u):
                p = proj[L]
                kind, m, c = UNITS[L][u]
                b = u % 4
                cs = slice(c * CH, (c + 1) * CH)
                if u >= 4:
                    pe.wait_ge(p.rem, u - 3)
                if kind == "kr":
                    for kc in range(KC):
                        ins = mm(ps[:, b, :], w_kr[:, kc, :], XT[:, kc, cs], kc == 0, kc == KC - 1)
                elif kind == "q":
                    pe.wait_ge(p.zq_sb, c + 1)
                    pe.wait_ge(p.rot, 6)
                    ins = mm(ps[:, b, :], w_uq[:, m * P:(m + 1) * P], cq_t[0:DQ, cs], True, True)
                elif kind == "kn":
                    pe.wait_ge(p.zkv_sb, c + 1)
                    ins = mm(ps[:, b, :], w_kn, ckv_t[:, cs], True, True)
                else:
                    for kc in range(KC):
                        ins = mm(ps[:, b, :], w_qkv[:, kc, m * P:(m + 1) * P], XT[:, kc, cs], kc == 0, kc == KC - 1)
                ins.then_inc(p.u_ps, 1)

            def v_products(L, v):
                p = proj[L]
                if L == 0 and v == 0:
                    pe.wait_ge(p.zkv_sb, NCH)
                if v >= 2:
                    pe.wait_ge(p.v_sb, v - 1)
                for t in range(2):
                    ts = slice((2 * v + t) * P, (2 * v + t + 1) * P)
                    o = ps[:, 6 + v % 2, t * C:(t + 1) * C]
                    if L == 0:
                        if v < 2:
                            pe.wait_ge(p.zq_sb, NCH)
                        ins = mm(o, ckv_t[:, ts], w_v0, True, True)
                    else:
                        for kc in range(KC):
                            ins = mm(o, XT[:, kc, ts], w_qkv[:, kc, 2 * C:3 * C], kc == 0, kc == KC - 1)
                ins.then_inc(p.v_ps, 1)

            pe.wait_ge(ident_in, 16)
            pe.wait_ge(setup_done, 4)
            for L in range(2):
                p = proj[L]
                for b in range(NCH - L):
                    transpose_batch(2 * L, b)
                pe.wait_ge(w_in[L], 16 * (7 if L == 0 else 2))
                if L == 0:
                    pe.wait_ge(turn[0].moved_a, NT // 2)

                def chunk_tensor(what, c):
                    p = proj[0]
                    for i in range(TPC * c, TPC * (c + 1)):
                        if what == "down":
                            if i >= 2:
                                pe.wait_ge(p.down_sb, i - 1)
                            for kc in range(KC):
                                ins = mm(ps[:, 4 + i % 2, 0:DQ + DKV], XT[:, kc, i * P:(i + 1) * P], w_down[:, kc, :],
                                         kc == 0, kc == KC - 1)
                            ins.then_inc(p.down_ps, 1)
                        else:
                            if i == TPC * c and c > 0:
                                pe.wait_ge(p.zq_sb, c)
                                pe.wait_ge(p.zkv_sb, c)
                            t = i - TPC * c
                            pe.wait_ge(p.z, 2 * i + 2)
                            pe.transpose(ps[0:DQ, 6, t * P:(t + 1) * P], c_down[:, i, 0:DQ], ident[:])
                            ins = pe.transpose(ps[:, 7, t * P:(t + 1) * P], c_down[:, i, DQ:DQ + DKV], ident[:])
                    if what == "zt":
                        ins.then_inc(p.zt_ps, 1)

                for u in range(NU):
                    for what, c in before(L, PE_BEFORE, u):
                        chunk_tensor(what, c)
                    if L == 1 and u in (0, 2, 4):
                        pe.wait_ge(turn[2].moved_a, 4 if u == 0 else 2 * (u // 2 + 1))
                        if u == 4:
                            pe.wait_ge(f.evac, NT)
                            transpose_batch(2, NCH - 1)
                            pe.wait_ge(turn[2].moved_a, NT // 2)
                    unit_products(L, u)
                    for v in v_after(L, u):
                        v_products(L, v)

                if L == 0:
                    pe.wait_ge(consts_in, 48)
                    pe.wait_ge(ones_done, 1)
                pe.wait_ge(p.rem, NU)
                pe.wait_ge(p.v_sb, VU)
                seen = set()
                n_half = 16 * 2 * len(STACK_RUNS)
                pe.wait_ge(stack_half[L], n_half)
                stepped = set()
                for o in ORDER:
                    if o.ring is not None and o.ring >= RING:
                        pe.wait_ge(s.ring_free, L * RING_N + o.ring - RING + 1)
                    if o.kind == "S":
                        if o.g not in seen and (o.g > 0 or o.Q >= NCH // 2):
                            seen.add(o.g)
                            pe.wait_ge(stack_in[L][o.g % 2], n_half * (HALF * (o.g // 2 + 1) - (o.g % 2 == 0)))
                        n = CH if o.c < o.Q else P * (o.r + 1)
                        bank = ps[:, RING0 + o.ring % RING, :]
                        ins = mm(bank[:, 0:n], q_stack[0:NSTACK, o.g % 2, o.Q // CPH, o.h, q_at(o) + o.r * P:q_at(o) + (o.r + 1) * P],
                                 k_stack[0:NSTACK, o.g % 2, o.c // CPH, o.h, o.c % CPH * CH:o.c % CPH * CH + n], True, True)
                        ins.then_inc(s.ring_filled, 1)
                    if o.kind == "MT":
                        pe.wait_ge(s.mparts, 4 * (L * NSTEP + o.n + 1))
                        pe.transpose(ps[:, RING0 + o.ring % RING, 0:P // 2].bitcast(BF16),
                                     m_parts[:, o.n % 2, :], ident_bf[:]).then_inc(s.ring_filled, 1)
                    if o.kind == "T":
                        if o.n not in stepped:
                            stepped.add(o.n)
                            pe.wait_ge(mrows_in[o.n % 2], L * MROWS_N + 16 * HG * (o.n // 2 + 1))
                        if o.k >= 2:
                            pe.wait_ge(s.exp_done, L * T_N + o.k - 1)
                        for h in range(2):
                            hh = 2 * o.hp + h
                            ins = mm(psT[:, o.k % 2, h, o.off:CH],
                                     k_stack[0:KROWS, o.g % 2, o.kt // KPH, hh, o.kt % KPH * P:(o.kt % KPH + 1) * P],
                                     q_stack[0:KROWS, o.g % 2, o.Q // CPH, hh, q_at(o) + o.off:q_at(o) + CH], True, True)
                        ins.then_inc(s.t_filled, 1)
                    if o.kind == "PV":
                        if o.sel is not None:
                            pe.wait_ge(s.selected, L * SEL_N + o.sel)
                        else:
                            pe.wait_ge(s.exp_done, L * T_N + 2 * o.j + 2)
                        if o.first:
                            pe.wait_ge(s.v_staged, L * NG + o.g + 1)
                            if o.n == 0:
                                pe.wait_ge(s.v_ones, L + 1)
                            if o.n > 0:
                                pe.wait_ge(s.y_evac, L * NSTEP + o.n)
                        for h in range(HG):
                            ins = mm(ps[32 * h:32 * h + VW, PV_BANK, o.off:CH], v_stage[:, o.g % 2, o.kt, h, :],
                                     probs[:, o.j % SLOTS, h, o.off:CH], o.first, o.last)
                        ins.then_inc(s.pv_done, 1)
                    if o.kind == "YT":
                        pe.wait_ge(s.y_evac, L * NSTEP + o.n + 1)
                        for r in range(TPC):
                            ins = pe.transpose(ps[:, RING0 + o.ring % RING, r * P:(r + 1) * P],
                                               y_chunk[:, o.n % 2, r * P:(r + 1) * P], ident[:])
                        ins.then_inc(s.ring_filled, 1)
                pe.wait_ge(s.ring_free, (L + 1) * RING_N)
                pe.wait_ge(s.exp_done, (L + 1) * T_N)

                q = oproj[L]

                def o_transpose(u):
                    if u >= 2:
                        pe.wait_ge(q.yt_sb, u - 1)
                    for t in range(2):
                        for kc in range(KC):
                            ins = pe.transpose(ps[:, u % 2, (2 * t + kc) * P:(2 * t + kc + 1) * P],
                                               Y[:, 2 * u + t, kc * P:(kc + 1) * P], ident[:])
                    ins.then_inc(q.yt_ps, 1)

                o_transpose(0)
                for u in range(NT // 2):
                    if u + 1 < NT // 2:
                        o_transpose(u + 1)
                    pe.wait_ge(q.yt_sb, u + 1)
                    if u >= 2:
                        pe.wait_ge(q.o_sb, 2 * (u - 1))
                    for t in range(2):
                        for kc in range(KC):
                            ins = mm(ps[:, 2 + u % 2, t * C:(t + 1) * C], y_t[:, u % 2, 2 * t + kc, :], w_o[:, kc, :],
                                     kc == 0, kc == KC - 1)
                    ins.then_inc(q.o_ps, 1)

                k1 = 1 + 2 * L
                transpose_batch(k1, 0)
                f = ffn[L]
                pe.wait_ge(wffn_done[L], 3)

                def down(u):
                    c, i = divmod(u, NI)
                    pe.wait_ge(f.lo, u + 1)
                    if i == 0 and c > 0:
                        pe.wait_ge(f.evac, TPC * c)
                    if i == 0:
                        for bank in (4, 5):
                            mm(ps[:, bank, :], zeros[:], w_gate[0:1, 0, 0:CH], True, False)
                    for t in range(TPC):
                        for k, part in enumerate((fuse_hi, frem_hi, flo_r)):
                            ins = mm(ps[:, 4 + t // 2, t % 2 * C:(t % 2 + 1) * C], part[:, u % 3, t * P:(t + 1) * P],
                                     w_dn[:, i, :], False, i == NI - 1 and k == 2 and t % 2 == 1)
                    ins.then_inc(f.down, 1)

                for u in range(NCH * NI):
                    c, i = divmod(u, NI)
                    if u >= 2:
                        pe.wait_ge(f.fuse, u - 1)
                    if i == 0:
                        pe.wait_ge(turn[k1].moved_v, 2 * c + 2)
                    for w, bank in ((w_gate, u % 2), (w_up, 2 + u % 2)):
                        for kc in range(KC):
                            for k in range(2):
                                ins = mm(ps[:, bank, :], w[:, kc, i * P:(i + 1) * P],
                                         x16[:, k, kc, c * CH:(c + 1) * CH], kc == 0 and k == 0,
                                         kc == KC - 1 and k == 1)
                    ins.then_inc(f.gu_ps, 1)
                    if u >= 2:
                        down(u - 2)
                    if i == XHAT_AT[c] + 2:
                        transpose_batch(k1, c + 1)
                down(NCH * NI - 2)
                down(NCH * NI - 1)
                pe.wait_ge(f.fuse, NCH * NI)


def kernel(**inputs):
    import concourse.bacc as bacc
    from concourse.bass_utils import run_bass_kernel_spmd

    w = {k: np.asarray(v) for k, v in inputs.items()}
    swap = np.arange(C).reshape(H, DH).copy()
    swap[:, DN:] = np.roll(swap[:, DN:], DR // 2, axis=1)
    swap = swap.reshape(-1)
    by_row = np.arange(C).reshape(2, H // 2, DH).transpose(0, 2, 1).reshape(-1)

    inv_freq = (np.float32(1.0 / 10000.0) ** (np.arange(0, DR, 2, dtype=np.float32) / np.float32(DR))).astype(np.float32)
    freqs = np.arange(H, dtype=np.float32)[:, None] * inv_freq[None, :]
    cos, sin = np.cos(freqs).astype(np.float32), np.sin(freqs).astype(np.float32)
    cos_row = np.concatenate([np.ones((H, DN), np.float32), cos, cos], axis=1).reshape(-1)
    sin_row = np.concatenate([np.zeros((H, DN), np.float32), sin, -sin], axis=1).reshape(-1)

    def tiles(a):
        return np.ascontiguousarray(a.reshape(-1, P, a.shape[1]).transpose(1, 0, 2))

    u_kv = w["L0_attn_W_u_kv"].reshape(H, DN + DH, DKV)
    b_ukv = w["L0_attn_b_u_kv"].reshape(H, DN + DH)
    cols = np.zeros((P, NCOLS), np.float32)
    cols[:DQ, 0], cols[:DQ, 1] = w["L0_attn_q_norm_g"], w["L0_attn_q_norm_b"]
    cols[:, 2], cols[:, 3] = w["L0_attn_kv_norm_g"], w["L0_attn_kv_norm_b"]
    cols[:, 4:6] = w["L0_attn_b_u_q"][by_row].reshape(2, P).T
    cols[:, 6:8] = w["L0_attn_b_u_q"][swap][by_row].reshape(2, P).T
    cols[:, 8] = b_ukv[:, :DN].T.reshape(-1)
    cols[:, 9] = np.repeat(w["L0_attn_b_d_kv"][DKV:], H)
    cos_row, sin_row = cos_row[by_row], sin_row[by_row]
    cols[:, 46:48], cols[:, 48:50] = cos_row.reshape(2, P).T, sin_row.reshape(2, P).T
    cols[:, 10:14] = w["L1_attn_b_qkv"][:2 * C].reshape(2, C)[:, by_row].reshape(4, P).T
    for L in range(2):
        cols[:, COLS["s_gate"][L]:COLS["s_gate"][L] + NI] = w[f"L{L}_ffn_s_gate"].reshape(NI, P).T
        cols[:, COLS["s_up"][L]:COLS["s_up"][L] + NI] = w[f"L{L}_ffn_s_up"].reshape(NI, P).T
    rows = np.concatenate([w["L0_attn_b_d_q"], w["L0_attn_b_d_kv"][:DKV], b_ukv[:, DN:].reshape(-1), w["L0_attn_b_o"],
                           w["L1_attn_b_qkv"][2 * C:], w["L1_attn_b_out"], w["L0_ffn_s_down"],
                           w["L1_ffn_s_down"]]).reshape(1, NROWS)
    bf = mybir.dt.np(BF16)
    arrays = {
        "x": w["L0_attn_x"].reshape(T, C),
        "cols": cols, "rows": rows, "rotary": np.concatenate([cos_row, sin_row]).reshape(1, 2 * C),
        "ident": np.eye(P, dtype=np.float32), "ident_bf": np.eye(P).astype(bf),
        "causal": np.concatenate([np.zeros((P, CH - P)), np.triu(np.full((P, P), MASKED), 1)], 1).astype(np.float32),
        "w_down": tiles(np.concatenate([w["L0_attn_W_d_q"], w["L0_attn_W_d_kv"][:DKV]]).T),
        "w_kr": tiles(np.repeat(w["L0_attn_W_d_kv"][DKV:], H, axis=0).T),
        "w_uq": np.ascontiguousarray(w["L0_attn_W_u_q"][by_row].T),
        "w_uq_swap": np.ascontiguousarray(w["L0_attn_W_u_q"][swap][by_row].T),
        "w_kn": np.ascontiguousarray(u_kv[:, :DN].transpose(1, 0, 2).reshape(H * DN, DKV).T),
        "w_v0": np.ascontiguousarray(u_kv[:, DN:].reshape(H * DH, DKV).T),
        "w_qkv": tiles(w["L1_attn_w_qkv"][np.concatenate([by_row, C + by_row, np.arange(2 * C, 3 * C)])].T),
        "w_o": np.stack([tiles(w["L0_attn_W_o"].T), tiles(w["L1_attn_w_out"].T)]),
    }
    for name, key in (("w_gate", "w_gate"), ("w_up", "w_up"), ("w_dn", "w_down")):
        arrays[name] = np.stack([tiles(w[f"L{L}_ffn_{key}"]).reshape(P, -1) for L in range(2)]).view(np.int32)

    nc = bacc.Bacc("TRN2", target_bir_lowering=False, num_devices=1)
    D = {k: nc.dram_tensor(f"in_{k}", v.shape, mybir.dt.from_np(v.dtype), kind="ExternalInput").ap()
         for k, v in arrays.items()}
    for name, shape in (("q_parts", (2, HALF, 3, DH, H // 2, TH)), ("k_parts0", (HALF, 3, DH, H, TH)),
                        ("k_parts1", (2, HALF, 3, DH, H // 2, TH))):
        D[name] = nc.dram_tensor(name, shape, BF16, kind="Internal").ap()
    out = nc.dram_tensor("out_dram", (T, C), F32, kind="ExternalOutput").ap()
    build_program(nc, D, out)
    got = run_bass_kernel_spmd(nc, [{f"in_{k}": v for k, v in arrays.items()}], core_ids=[0])
    return got.results[0]["out_dram"].reshape(1, T, C)
```
